# Optimizing a Trainium2 kernel written in Bass

```python
import numpy as np
import jax
import jax.numpy as jnp

def _softmax(x, axis=-1):
    return jax.nn.softmax(x, axis=axis)

def _gelu(x):
    return jax.nn.gelu(x, approximate=True)

def _silu(x):
    return jax.nn.silu(x)

def _sigmoid(x):
    return jax.nn.sigmoid(x)

def _layernorm(x, axis=-1, eps=1e-05):
    m = jnp.mean(x, axis=axis, keepdims=True)
    v = jnp.var(x, axis=axis, keepdims=True)
    return (x - m) / jnp.sqrt(v + eps)

def _scatter_add(tgt, idx, src, axis=0):
    return tgt.at[idx].add(src)

def _segment_sum(src, seg, n):
    return jax.ops.segment_sum(src, seg, n)
kernel_name = 'mk_flamingo_gated_d1_seqx_r2_28b499'

def setup_inputs(seed: int=0):
    np.random.seed(seed)
    _w = jnp.asarray

    def _rec_inputs():
        import jax
        import jax.numpy as jnp
        _rk = jax.random.key(seed)
        x = -0.0002928 + 1 * jax.random.normal(jax.random.fold_in(_rk, 1), (8, 512, 512), jnp.float32)
        _lenS = 512 - jax.random.randint(jax.random.fold_in(_rk, 7), (8,), 0, max(1, 512 // 4) + 1, jnp.int32)
        _lenS2 = 77 - jax.random.randint(jax.random.fold_in(_rk, 8), (8,), 0, max(1, 77 // 4) + 1, jnp.int32)
        _ctx_768P = jax.random.normal(jax.random.fold_in(_rk, 11), (8, 16, 384), jnp.float32)
        _ctx_768c = jax.random.dirichlet(jax.random.fold_in(_rk, 511), 0.3 * jnp.ones((16,), jnp.float32), (8, 77))
        _ctx_768t = jnp.einsum('bsk,bkd->bsd', _ctx_768c, _ctx_768P)
        _ctx_768t = _ctx_768t * jax.lax.rsqrt(jnp.mean(jnp.square(_ctx_768t)) + 1e-12) * 0.953939
        ctx_768 = 2.09791e-05 + 1.00001 * (_ctx_768t + 0.3 * jax.random.normal(jax.random.fold_in(_rk, 611), (8, 77, 384), jnp.float32))
        _validS = jnp.arange(512)[None, :] < _lenS[:, None]
        _validS2 = jnp.arange(77)[None, :] < _lenS2[:, None]
        _causal = jnp.tril(jnp.ones((512, 512), dtype=bool))
        mask_BxS2_bf1 = jnp.ones((8, 77), dtype=bool)
        _g = jax.random.normal(jax.random.fold_in(_rk, 9001), (2, 1), jnp.float32)
        _g = jnp.sign(_g) * jnp.maximum(jnp.abs(_g), 1.0) + (_g == 0) * 1.0
        g_xattn = _g[0]
        g_ffn = _g[1]
        return (x, ctx_768, mask_BxS2_bf1, g_xattn, g_ffn)
    x, ctx_768, mask_BxS2_bf1, g_xattn, g_ffn = _rec_inputs()

    def _L0_xattn_setup():
        import jax, jax.numpy as jnp
        import numpy as np
        import math
        B, N, M = (4, 512, 512)
        DIM, CTX_DIM = (512, 384)
        HEADS, DIM_HEAD = (16, 64)
        INNER = HEADS * DIM_HEAD

        def layer_norm(t, g, eps=1e-05):
            mean = jnp.mean(t, axis=-1, keepdims=True)
            var = jnp.mean((t - mean) ** 2, axis=-1, keepdims=True)
            return (t - mean) * jax.lax.rsqrt(var + eps) * g
        key = jax.random.key(seed)
        ks = jax.random.split(key, 8)
        return {'x': jax.random.normal(ks[0], (B, N, DIM), jnp.float32), 'context': jax.random.normal(ks[1], (B, M, CTX_DIM), jnp.float32), 'mask': jnp.ones((B, M), dtype=bool), 'g_norm': jnp.ones((DIM,), jnp.float32), 'null_kv': jax.random.normal(ks[2], (2, DIM_HEAD), jnp.float32), 'Wq': jax.random.normal(ks[3], (DIM, INNER), jnp.float32) * DIM ** (-0.5), 'Wkv': jax.random.normal(ks[4], (CTX_DIM, 2 * INNER), jnp.float32) * CTX_DIM ** (-0.5), 'Wout': jax.random.normal(ks[5], (INNER, DIM), jnp.float32) * INNER ** (-0.5), 'g_out': jnp.ones((DIM,), jnp.float32)}
    _L0_xattn_all = _L0_xattn_setup()
    _L0_xattn_in = {k: v for k, v in _L0_xattn_all.items() if k in ('g_norm', 'null_kv', 'Wq', 'Wkv', 'Wout', 'g_out')}
    del _L0_xattn_all

    def _L0_ffn_setup():
        import jax, jax.numpy as jnp
        import numpy as np
        NUM_OPS, B, T, D = (8, 8, 256, 512)
        key = jax.random.key(seed)
        k1, k2, k3, k4 = jax.random.split(key, 4)
        x = jax.random.normal(k1, (B, T, D), dtype=jnp.float32)
        W = jax.random.normal(k2, (NUM_OPS, D, D), dtype=jnp.float32) * 0.02
        b = jnp.zeros((NUM_OPS, D), dtype=jnp.float32)
        logits = 0.001 * jax.random.normal(k3, (NUM_OPS,), dtype=jnp.float32)
        u = jax.random.uniform(k4, (NUM_OPS,), dtype=jnp.float32, minval=1e-06, maxval=1.0 - 1e-06)
        return {'x': x, 'W': W, 'b': b, 'logits': logits, 'u': u}
    _L0_ffn_all = _L0_ffn_setup()
    _L0_ffn_in = {k: v for k, v in _L0_ffn_all.items() if k in ('W', 'b', 'logits', 'u')}
    del _L0_ffn_all
    return {'x': x, 'ctx_768': ctx_768, 'mask_BxS2_bf1': mask_BxS2_bf1, 'g_xattn': g_xattn, 'g_ffn': g_ffn, 'L0_xattn_g_norm': _L0_xattn_in['g_norm'], 'L0_xattn_null_kv': _L0_xattn_in['null_kv'], 'L0_xattn_Wq': _L0_xattn_in['Wq'], 'L0_xattn_Wkv': _L0_xattn_in['Wkv'], 'L0_xattn_Wout': _L0_xattn_in['Wout'], 'L0_xattn_g_out': _L0_xattn_in['g_out'], 'L0_ffn_W': _L0_ffn_in['W'], 'L0_ffn_b': _L0_ffn_in['b'], 'L0_ffn_logits': _L0_ffn_in['logits'], 'L0_ffn_u': _L0_ffn_in['u']}

def reference(x, ctx_768, mask_BxS2_bf1, g_xattn, g_ffn, L0_xattn_g_norm, L0_xattn_null_kv, L0_xattn_Wq, L0_xattn_Wkv, L0_xattn_Wout, L0_xattn_g_out, L0_ffn_W, L0_ffn_b, L0_ffn_logits, L0_ffn_u):
    import jax
    import jax.numpy as jnp

    def _L0_xattn_ref(x, context, mask, g_norm, null_kv, Wq, Wkv, Wout, g_out):
        import jax, jax.numpy as jnp
        import numpy as np
        import math
        B, N, M = (4, 512, 512)
        DIM, CTX_DIM = (512, 384)
        HEADS, DIM_HEAD = (16, 64)
        INNER = HEADS * DIM_HEAD

        def layer_norm(t, g, eps=1e-05):
            mean = jnp.mean(t, axis=-1, keepdims=True)
            var = jnp.mean((t - mean) ** 2, axis=-1, keepdims=True)
            return (t - mean) * jax.lax.rsqrt(var + eps) * g
        b = x.shape[0]
        scale = DIM_HEAD ** (-0.5)
        sqrt_scale = math.sqrt(scale)
        x = layer_norm(x, g_norm)
        q = x @ Wq
        kv = context @ Wkv
        k, v = jnp.split(kv, 2, axis=-1)

        def to_heads(t):
            return t.reshape(b, t.shape[1], HEADS, DIM_HEAD).transpose(0, 2, 1, 3)
        q, k, v = (to_heads(q), to_heads(k), to_heads(v))
        nk = jnp.broadcast_to(null_kv[0], (b, HEADS, 1, DIM_HEAD))
        nv = jnp.broadcast_to(null_kv[1], (b, HEADS, 1, DIM_HEAD))
        k = jnp.concatenate([nk, k], axis=2)
        v = jnp.concatenate([nv, v], axis=2)
        q = q * sqrt_scale
        k = k * sqrt_scale
        sim = jnp.einsum('bhid,bhjd->bhij', q, k)
        max_neg = -jnp.finfo(sim.dtype).max
        full_mask = jnp.pad(mask, ((0, 0), (1, 0)), constant_values=True)
        sim = jnp.where(full_mask[:, None, None, :], sim, max_neg)
        attn = jax.nn.softmax(sim.astype(jnp.float32), axis=-1).astype(sim.dtype)
        out = jnp.einsum('bhij,bhjd->bhid', attn, v)
        out = out.transpose(0, 2, 1, 3).reshape(b, -1, INNER)
        out = out @ Wout
        return layer_norm(out, g_out)

    def _L0_ffn_ref(x, W, b, logits, u):
        import jax, jax.numpy as jnp
        import numpy as np
        NUM_OPS, B, T, D = (8, 8, 256, 512)
        gumbel = -jnp.log(-jnp.log(u))
        idx = jnp.argmax(jax.nn.log_softmax(logits) + gumbel)
        out = jnp.einsum('btd,de->bte', x, W[idx]) + b[idx]
        return out
    x = x + jnp.tanh(g_xattn[0]) * _L0_xattn_ref(_layernorm(x, axis=-1), ctx_768, mask_BxS2_bf1, L0_xattn_g_norm, L0_xattn_null_kv, L0_xattn_Wq, L0_xattn_Wkv, L0_xattn_Wout, L0_xattn_g_out)
    x = x + jnp.tanh(g_ffn[0]) * _L0_ffn_ref(_layernorm(x, axis=-1), L0_ffn_W, L0_ffn_b, L0_ffn_logits, L0_ffn_u)
    return x

_drawn_inputs = setup_inputs


def setup_inputs(seed=0):
    import zlib

    import numpy as np

    out = dict(_drawn_inputs(seed))
    spreads = {'L0_xattn_g_norm': (1.0, 0.2), 'L0_xattn_g_out': (1.0, 0.2), 'L0_ffn_b': (0.0, 0.1)}
    factors = {}
    for name, (base, spread) in spreads.items():
        noise = np.random.default_rng([zlib.crc32(name.encode()), seed]).standard_normal(out[name].shape)
        drawn = base * np.exp(spread * noise) if base else spread * noise
        out[name] = jnp.asarray(drawn.astype(out[name].dtype))
    for name, factor in factors.items():
        out[name] = (out[name] * factor).astype(out[name].dtype)
    return out
```

```python
from contextlib import ExitStack

import concourse.bass as bass
from concourse import mybir

F32 = mybir.dt.float32
F32R = mybir.dt.float32r
U32 = mybir.dt.uint32
U8 = mybir.dt.uint8
ALU = mybir.AluOpType
ACT = mybir.ActivationFunctionType
AX = mybir.AxisListType

P = 128
EPS = 1e-5
MASKED = 3.0e38
DH = 64


def flamingo_program(nc, x, ctx_t, mask, g_xattn, g_ffn, g_norm, null_kv, w_q, w_kv, w_out, g_out,
                     ffn_w, ffn_b, ffn_logits, ffn_u, out):
    B, N, D = x.shape
    C, BJ = ctx_t.shape
    J = BJ // B
    JN = J + 1
    INNER = w_q.shape[1]
    E = ffn_w.shape[0]
    TT = N // P
    DC = D // P
    CC = C // P
    NU = INNER // P
    HALF = NU // 2
    W2 = 2 * JN
    JH = BJ // 2
    VT = (BJ + P - 1) // P
    assert (TT, DC, NU) == (4, 4, 8) and N == 512 and D == 512 and BJ % 2 == 0

    x_tok = x.rearrange("b n d -> (b n) d")
    out_tok = out.rearrange("b n d -> (b n) d")

    stack = ExitStack()

    def sb(name, shape, dt=F32):
        return stack.enter_context(nc.sbuf_tensor(name, shape, dt))

    def sem(name):
        return stack.enter_context(nc.semaphore(name))

    k_dram = nc.dram_tensor("k_dram", (2, INNER, BJ), F32, kind="Internal").ap()
    v_dram = nc.dram_tensor("v_dram", (BJ, INNER), F32, kind="Internal").ap()

    with stack:
        ps = stack.enter_context(nc.psum_tensor("ps", [P, 8, 512], F32))
        SCORE, WORK = 4, 5

        wq_hi = sb("wq_hi", [P, DC, INNER], F32R)
        wq_lo = sb("wq_lo", [P, DC, INNER], F32R)
        xt_hi = sb("xt_hi", [P, 2, DC, N], F32R)
        xt_lo = sb("xt_lo", [P, 2, DC, N], F32R)
        k_bd = sb("k_bd", [P, 2, NU, W2], F32R)
        v_sb = sb("v_sb", [JN, INNER])
        xin = sb("xin", [P, TT, D])
        stage = sb("stage", [P, 3, 1024])
        gout = sb("gout", [P, D])
        bias = sb("bias", [P, D])
        mask_bias = sb("mask_bias", [P, B, JN])
        ident = sb("ident", [P, P])
        gn = sb("gn", [P, DC])
        half_neg = sb("half_neg", [P, TT])
        gates = sb("gates", [P, 2])
        tanh_g = sb("tanh_g", [P, 2])
        null_k = sb("null_k", [P, 1])
        route = sb("route", [1, 10, 8])
        route_i = sb("route_i", [1, 8], U32)
        x_stat = sb("x_stat", [P, TT, 6])
        x_mv = sb("x_mv", [P, TT, 2])
        x_var = sb("x_var", [P, TT])
        x_rstd = sb("x_rstd", [P, TT])
        y_stat = sb("y_stat", [P, TT, 6])
        y_mv = sb("y_mv", [P, TT, 2])
        y_var = sb("y_var", [P, TT])
        y_rstd = sb("y_rstd", [P, TT])
        y_nmr = sb("y_nmr", [P, TT])
        z_stat = sb("z_stat", [P, TT, 6])
        z_mv = sb("z_mv", [P, TT, 2])
        z_var = sb("z_var", [P, TT])
        z_rstd = sb("z_rstd", [P, TT])
        z_nmr = sb("z_nmr", [P, TT])
        s_top = sb("s_top", [P, 2 * TT])
        s_sum = sb("s_sum", [P, 2 * TT])
        s_rcp = sb("s_rcp", [P, 2 * TT])

        early = ExitStack()
        with early:
            def esb(name, shape, dt=F32):
                return early.enter_context(nc.sbuf_tensor(name, shape, dt))
            wkv_hi = esb("wkv_hi", [P, 2, CC, INNER], F32R)
            wkv_lo = esb("wkv_lo", [P, 2, CC, INNER], F32R)
            ctx_hi = esb("ctx_hi", [P, CC, BJ], F32R)
            ctx_lo = esb("ctx_lo", [P, CC, BJ], F32R)
            ctx_in = esb("ctx_in", [P, CC, BJ])
            k_st = esb("k_st", [P, 2, 2, BJ], F32R)
            v_st = esb("v_st", [P, 2, INNER])
        wo_hi = sb("wo_hi", [P, NU, D], F32R)
        wo_lo = sb("wo_lo", [P, NU, D], F32R)
        wf_hi = sb("wf_hi", [P, DC, D], F32R)
        wf_lo = sb("wf_lo", [P, DC, D], F32R)
        p_t = sb("p_t", [JN, 2, N])
        o_hi = sb("o_hi", [P, N], F32R)
        o_lo = sb("o_lo", [P, N], F32R)
        prob = sb("prob", [P, 2, 2 * TT, JN])
        q_hi = sb("q_hi", [P, N], F32R)
        q_lo = sb("q_lo", [P, N], F32R)
        zn = sb("zn", [P, 2, D])
        zt_hi = sb("zt_hi", [P, 2, DC, P], F32R)
        zt_lo = sb("zt_lo", [P, 2, DC, P], F32R)
        row = sb("row", [P, TT, D])
        x_res = sb("x_res", [P, TT, D])
        mask_u8 = sb("mask_u8", [P, B * J], U8)

        s_ctx_in = sem("s_ctx_in")
        s_const_in = sem("s_const_in")
        s_route_in = sem("s_route_in")
        s_stage_in = [sem(f"s_stage_in{i}") for i in range(3)]
        s_x_in = [sem(f"s_x_in{t}") for t in range(TT)]
        s_res_in = sem("s_res_in")
        s_bias_in = sem("s_bias_in")
        s_k_in = [sem(f"s_k_in{h}") for h in range(2)]
        s_v_in = [sem(f"s_v_in{h}") for h in range(2)]
        s_k_out = [sem(f"s_k_out{i}") for i in range(2)]
        s_v_out = [sem(f"s_v_out{i}") for i in range(2)]
        s_null_in = sem("s_null_in")
        s_null_v = sem("s_null_v")
        s_out = sem("s_out")
        s_ident = sem("s_ident")
        s_tanh = sem("s_tanh")
        s_ra = sem("s_ra")
        s_rd = sem("s_rd")
        s_expert = sem("s_expert")
        s_ctx_hi = sem("s_ctx_hi")
        s_ctx_lo = sem("s_ctx_lo")
        s_w_hi = sem("s_w_hi")
        s_w_lo = sem("s_w_lo")
        s_k_mm = sem("s_k_mm")
        s_k_hi = sem("s_k_hi")
        s_k_lo = sem("s_k_lo")
        s_v_mm = sem("s_v_mm")
        s_v_act = sem("s_v_act")
        s_v_dve = sem("s_v_dve")
        s_kz = sem("s_kz")
        s_null_hi = sem("s_null_hi")
        s_null = sem("s_null")
        s_mask = sem("s_mask")
        s_gout = sem("s_gout")
        s_bias = sem("s_bias")
        s_q_mm = sem("s_q_mm")
        s_s_mm = sem("s_s_mm")
        s_pt_mm = sem("s_pt_mm")
        s_pv_mm = sem("s_pv_mm")
        s_y_mm = sem("s_y_mm")
        s_xt_mm = sem("s_xt_mm")
        s_zt_mm = sem("s_zt_mm")
        s_f_mm = sem("s_f_mm")
        s_q_hi = sem("s_q_hi")
        s_exp = sem("s_exp")
        s_pt = sem("s_pt")
        s_o_hi = sem("s_o_hi")
        s_xt_hi = sem("s_xt_hi")
        s_yn = sem("s_yn")
        s_zn = sem("s_zn")
        s_zt_hi = sem("s_zt_hi")
        s_q_lo = sem("s_q_lo")
        s_masked = sem("s_masked")
        s_top_ok = sem("s_top_ok")
        s_sum_ok = sem("s_sum_ok")
        s_rcp_ok = sem("s_rcp_ok")
        s_o_lo = sem("s_o_lo")
        s_xt_lo = sem("s_xt_lo")
        s_x_bn = sem("s_x_bn")
        s_x_mv = sem("s_x_mv")
        s_x_var = sem("s_x_var")
        s_y_bn = sem("s_y_bn")
        s_y_mv = sem("s_y_mv")
        s_y_var = sem("s_y_var")
        s_y_nmr = sem("s_y_nmr")
        s_x1 = sem("s_x1")
        s_z_bn = sem("s_z_bn")
        s_z_mv = sem("s_z_mv")
        s_z_var = sem("s_z_var")
        s_z_nmr = sem("s_z_nmr")
        s_zt_lo = sem("s_zt_lo")
        s_res = sem("s_res")
        s_sub = sem("s_sub")
        s_prob = sem("s_prob")
        s_x_rstd = sem("s_x_rstd")
        s_xn = sem("s_xn")
        s_y_rstd = sem("s_y_rstd")
        s_yg = sem("s_yg")
        s_z_rstd = sem("s_z_rstd")
        s_x1b = sem("s_x1b")

        chunks = [w_kv[c * P:(c + 1) * P, h * INNER:(h + 1) * INNER] for h in range(2) for c in range(CC)]
        chunks += [w_q[c * P:(c + 1) * P, :] for c in range(DC)]
        chunks += [w_out[2 * c * P:2 * (c + 1) * P, :].rearrange("(a p) d -> p a d", p=P) for c in range(NU // 2)]
        W_K, W_V, W_Q, W_O = 0, CC, 2 * CC, 2 * CC + DC
        W_F = W_O + NU // 2
        W_END = W_F + DC // 2

        def stage_of(n):
            s = stage[:, n % 3, :]
            return s if n < W_O else s.rearrange("p (a d) -> p a d", a=2)

        def parts_of(n):
            if n < W_Q:
                return wkv_hi[:, n // CC, n % CC, :], wkv_lo[:, n // CC, n % CC, :], None
            if n < W_O:
                c = n - W_Q
                return wq_hi[:, c, :], wq_lo[:, c, :], gn[:, c:c + 1]
            if n < W_F:
                c = 2 * (n - W_O)
                return wo_hi[:, c:c + 2, :], wo_lo[:, c:c + 2, :], None
            c = 2 * (n - W_F)
            return wf_hi[:, c:c + 2, :], wf_lo[:, c:c + 2, :], tanh_g[:, 1:2]

        def when(engine, semaphore, count):
            if not isinstance(count, int) or count > 0:
                engine.wait_ge(semaphore, count)

        def splits_in(b, u):
            if isinstance(b, int) and b == 0:
                return {0: [W_O], 1: [W_O + 1, W_O + 2], 2: [W_O + 3], 4: [W_F], 5: [W_F + 1]}.get(u, [])
            return []

        def run(engine, slot):
            for u in range(NU):
                slot(0, u)
            with engine.Fori(1, B - 1) as b:
                for u in range(NU):
                    slot(b, u)
            for u in range(NU):
                slot(B - 1, u)
            for u in range(NU):
                slot(B, u)

        def has(b):
            if isinstance(b, int):
                return b < B, b + 1 < B, b > 0
            return True, True, True

        def unit_back(b, u, lag):
            there = not isinstance(b, int) or 0 <= NU * b + u - lag < NU * B
            return there, (u - lag) % NU

        psum_scores = ps[:, SCORE, 0:2 * W2].rearrange("p (g j) -> p g j", j=JN)

        block = stack.enter_context(nc.Block())

        @block.sync
        def _(sp):
            def load_stage(n, src):
                if n >= 3:
                    sp.wait_ge(s_w_lo, n - 2)
                sp.dma_start(stage_of(n), src).then_inc(s_stage_in[n % 3], 16)

            def load_keys(b, h):
                for part in range(2):
                    for e in range(2):
                        src = k_dram[part, h * HALF * P:(h + 1) * HALF * P, bass.ds(b * J, J)]
                        src = src.rearrange("(u e d) j -> e d u j", u=HALF, e=2)[e]
                        dst = k_bd[DH * e:DH * (e + 1), part, h * HALF:(h + 1) * HALF, JN * e:JN * e + J]
                        sp.dma_start(dst.bitcast(F32), src).then_inc(s_k_in[h], 16)

            def load_values(b, h):
                cols = slice(h * HALF * P, (h + 1) * HALF * P)
                sp.dma_start(v_sb[0:J, cols], v_dram[bass.ds(b * J, J), cols]).then_inc(s_v_in[h], 16)

            def load_x(b, t):
                sp.dma_start(xin[:, t, :], x_tok[bass.ds(b * N + t * P, P), :]).then_inc(s_x_in[t], 16)

            sp.dma_start(ctx_in[:], ctx_t.rearrange("(c p) j -> p c j", p=P)).then_inc(s_ctx_in, 16)
            for n in range(3):
                load_stage(n, chunks[n])
            sp.dma_start(gn[:], g_norm).then_inc(s_const_in, 16)
            for t in range(TT):
                load_x(0, t)
            for n in range(3, W_Q + 1):
                load_stage(n, chunks[n])
            later = list(range(W_Q + 1, W_O))
            for c in range(NU):
                sp.wait_ge(s_k_lo, 2 * (c + 1))
                for part in range(2):
                    sp.dma_start(k_dram[part, c * P:(c + 1) * P, :], k_st[:, c % 2, part, :].bitcast(F32))\
                        .then_inc(s_k_out[c % 2], 16)
                if later:
                    load_stage(later[0], chunks[later.pop(0)])
            sp.wait_ge(s_kz, 2)
            for i in range(2):
                sp.wait_ge(s_k_out[i], 32 * (NU // 2))
            for h in range(2):
                load_keys(0, h)
            for m in range(VT):
                rows = min(P, BJ - m * P)
                sp.wait_ge(s_v_act, m + 1)
                sp.wait_ge(s_v_dve, m + 1)
                sp.dma_start(v_dram[m * P:m * P + rows, :], v_st[0:rows, m % 2, :]).then_inc(s_v_out[m % 2], 16)
            for n in range(W_O, W_O + 2):
                load_stage(n, chunks[n])
            sp.wait_ge(s_v_out[0], 16 * ((VT + 1) // 2))
            sp.wait_ge(s_v_out[1], 16 * (VT // 2))
            for h in range(2):
                load_values(0, h)
            sp.wait_ge(s_expert, 1)
            expert = sp.value_load(route_i[0:1, 0:1], min_val=0, max_val=E - 1)
            sp.dma_start(bias[:], ffn_b[bass.ds(expert, 1), :].partition_broadcast(P)
                         .rearrange("p a d -> p (a d)")).then_inc(s_bias_in, 16)
            for t in range(TT):
                sp.wait_ge(s_xt_mm, t + 1)
                load_x(1, t)
            load_stage(W_O + 2, chunks[W_O + 2])
            load_stage(W_O + 3, chunks[W_O + 3])
            for c in range(DC // 2):
                src = ffn_w[bass.ds(expert, 1), 2 * c * P:2 * (c + 1) * P, :]
                load_stage(W_F + c, src.rearrange("a (c p) d -> p (a c) d", p=P))

            def batch(b):
                cur, nxt, prev = has(b)
                if nxt and not (isinstance(b, int) and b == 0):
                    for t in range(TT):
                        when(sp, s_xt_mm, TT * b + t + 1)
                        load_x(b + 1, t)
                if cur and prev:
                    when(sp, s_pv_mm, NU * b)
                    load_values(b, 1)
                if nxt:
                    when(sp, s_s_mm, 2 * (NU * b + HALF))
                    load_keys(b + 1, 0)
                    when(sp, s_pv_mm, NU * b + HALF)
                    load_values(b + 1, 0)
                    when(sp, s_s_mm, 2 * (NU * b + NU))
                    load_keys(b + 1, 1)
                if prev:
                    for t in range(TT):
                        when(sp, s_res, TT * (b - 1) + t + 1)
                        sp.dma_start(out_tok[bass.ds((b - 1) * N + t * P, P), :], row[:, t, :])\
                            .then_inc(s_out, 16)
                if cur:
                    if prev:
                        when(sp, s_out, 16 * TT * b)
                    sp.dma_start(x_res[:], x_tok[bass.ds(b * N, N), :].rearrange("(t p) d -> p t d", p=P))\
                        .then_inc(s_res_in, 16)

            batch(0)
            with sp.Fori(1, B - 1) as b:
                batch(b)
            batch(B - 1)
            batch(B)
            sp.wait_ge(s_out, 16 * TT * B)

        @block.tensor
        def _(pe):
            def three(out_ap, terms, first, last):
                mm = None
                for n, (a_hi, a_lo, b_hi, b_lo) in enumerate(terms):
                    pe.matmul(out_ap, a_hi, b_hi, start=(first and n == 0), stop=False)
                    pe.matmul(out_ap, a_lo, b_hi, start=False, stop=False)
                    mm = pe.matmul(out_ap, a_hi, b_lo, start=False, stop=(last and n == len(terms) - 1))
                return mm

            def turn_x(b, t, bank):
                pe.wait_ge(s_ident, 2)
                when(pe, s_xn, TT * b + t + 1)
                for c in range(DC):
                    mm = pe.transpose(ps[:, bank, c * P:(c + 1) * P], xin[:, t, c * P:(c + 1) * P], ident[:])
                mm.then_inc(s_xt_mm, 1)

            pe.wait_ge(s_ctx_lo, 1)
            pe.wait_ge(s_w_lo, CC)
            for j in range(2 * NU):
                c, h = j // 2, j % 2
                when(pe, s_k_lo, j - 7)
                cols, toks = slice(c * P, (c + 1) * P), slice(h * JH, (h + 1) * JH)
                three(ps[:, j % 8, 0:JH],
                      [(wkv_hi[:, 0, k, cols], wkv_lo[:, 0, k, cols], ctx_hi[:, k, toks], ctx_lo[:, k, toks])
                       for k in range(CC)], True, True).then_inc(s_k_mm, 1)
            for t in range(TT):
                pe.wait_ge(s_k_lo, 9 + t)
                turn_x(0, t, t)
            pe.wait_ge(s_w_lo, 2 * CC)
            for n in range(2 * VT):
                m, h = n // 2, n % 2
                rows = min(P, BJ - m * P)
                if n < 4:
                    pe.wait_ge(s_k_lo, 13 + n)
                elif n < 8:
                    pe.wait_ge(s_xt_lo, n - 3)
                else:
                    pe.wait_ge((s_v_act, s_v_dve)[h], m - 3)
                toks, cols = slice(m * P, m * P + rows), slice(h * 512, (h + 1) * 512)
                three(ps[0:rows, (4 + n) % 8, :],
                      [(ctx_hi[:, k, toks], ctx_lo[:, k, toks], wkv_hi[:, 1, k, cols], wkv_lo[:, 1, k, cols])
                       for k in range(CC)], True, True).then_inc(s_v_mm, 1)
            pe.wait_ge(s_v_act, VT)
            pe.wait_ge(s_v_dve, VT)
            pe.wait_ge(s_w_lo, W_O)

            def scores(b, u, half):
                for tt in range(2):
                    toks = slice((2 * half + tt) * P, (2 * half + tt + 1) * P)
                    mm = three(ps[:, SCORE, tt * W2:(tt + 1) * W2],
                               [(q_hi[:, toks], q_lo[:, toks], k_bd[:, 0, u, :], k_bd[:, 1, u, :])], True, True)
                mm.then_inc(s_s_mm, 1)

            def turn_z(b, t, bank):
                when(pe, s_zn, TT * (b - 1) + t + 1)
                for c in range(DC):
                    mm = pe.transpose(ps[:, bank, c * P:(c + 1) * P], zn[:, t % 2, c * P:(c + 1) * P], ident[:])
                mm.then_inc(s_zt_mm, 1)

            def feed_forward(b, t, bank):
                when(pe, s_zt_lo, TT * (b - 1) + t + 1)
                i = t % 2
                three(ps[:, bank, :], [(zt_hi[:, i, c, :], zt_lo[:, i, c, :], wf_hi[:, c, :], wf_lo[:, c, :])
                                       for c in range(DC)], True, True).then_inc(s_f_mm, 1)

            def slot(b, u):
                cur, nxt, prev = has(b)
                g = b * NU + u
                pv, vu = unit_back(b, u, 2)
                yv, yu = unit_back(b, u, 3)
                tail = not cur
                if cur:
                    if prev and u in (5, 6, 7):
                        when(pe, *{5: (s_zt_lo, TT * (b - 1) + 1), 6: (s_res, TT * (b - 1) + 1),
                                   7: (s_res, TT * (b - 1) + 2)}[u])
                    if u == 0:
                        when(pe, s_xt_lo, TT * (b + 1))
                    par = b % 2
                    cols = slice(u * P, (u + 1) * P)
                    three(ps[:, WORK, :], [(wq_hi[:, c, cols], wq_lo[:, c, cols], xt_hi[:, par, c, :], xt_lo[:, par, c, :])
                                           for c in range(DC)], True, True).then_inc(s_q_mm, 1)
                if pv:
                    when(pe, s_masked, 2 * g if cur else 2 * NU * B)
                    if tail:
                        when(pe, s_o_lo, g - 2)
                    when(pe, s_prob, g - 1)
                    for e in range(2):
                        for t in range(TT):
                            mm = pe.transpose(ps[0:JN, WORK + 1 + e, t * P:(t + 1) * P],
                                              prob[:, u % 2, 2 * t + e, :], ident[:])
                        mm.then_inc(s_pt_mm, 1)
                if yv:
                    when(pe, s_o_lo, g - 2)
                    if isinstance(b, int) and b == 0 and yu == 0:
                        pe.wait_ge(s_w_lo, W_F)
                    for t in range(TT):
                        if yu == 0 and prev:
                            when(pe, s_yn, TT * (b - 1) + t + 1)
                        toks = slice(t * P, (t + 1) * P)
                        three(ps[:, t, :], [(o_hi[:, toks], o_lo[:, toks], wo_hi[:, yu, :], wo_lo[:, yu, :])],
                              yu == 0, yu == NU - 1).then_inc(s_y_mm, 1)
                if cur:
                    if u % HALF == 0:
                        when(pe, s_k_in[u // HALF], 64 * (b + 1))
                        if isinstance(b, int) and b == 0:
                            pe.wait_ge(s_null, 1)
                    if u < 2 and not pv:
                        when(pe, s_masked, 2 * g)
                    when(pe, s_q_lo, g + 1)
                    scores(b, u, 0)
                if pv:
                    when(pe, s_pt, 2 * (g - 1))
                    if vu % HALF == 0:
                        vb = b if u >= 2 else b - 1
                        when(pe, s_v_in[vu // HALF], 16 * (vb + 1))
                        if isinstance(b, int) and b == 0:
                            pe.wait_ge(s_null_v, 16)
                    for e in range(2):
                        cols = slice(vu * P + e * DH, vu * P + (e + 1) * DH)
                        mm = pe.matmul(ps[DH * e:DH * (e + 1), WORK + 1, :], v_sb[:, cols], p_t[:, e, :],
                                       start=True, stop=True)
                    mm.then_inc(s_pv_mm, 1)
                if nxt and 1 <= u < TT:
                    turn_x(b + 1, u - 1, WORK + 2)
                if prev:
                    if u == 4:
                        turn_z(b, 0, WORK)
                    if u == 5:
                        turn_z(b, 1, WORK + 2)
                        if isinstance(b, int) and b == 1 or not isinstance(b, int):
                            pe.wait_ge(s_w_lo, W_END)
                        if tail:
                            when(pe, s_zt_lo, TT * (b - 1) + 1)
                        feed_forward(b, 0, WORK)
                        when(pe, s_zt_lo, TT * (b - 1) + 2)
                        turn_z(b, 2, WORK + 2)
                    if u == 6:
                        if tail:
                            when(pe, s_res, TT * (b - 1) + 1)
                        feed_forward(b, 1, WORK)
                        if tail:
                            when(pe, s_zt_lo, TT * (b - 1) + 3)
                        turn_z(b, 3, WORK + 2)
                    if u == 7:
                        if tail:
                            when(pe, s_zt_lo, TT * (b - 1) + 4)
                        feed_forward(b, 2, WORK + 2)
                        if cur:
                            when(pe, s_o_lo, g - 1)
                        feed_forward(b, 3, WORK + 1)
                if nxt and u == TT:
                    turn_x(b + 1, u - 1, WORK + 2)
                if cur:
                    when(pe, s_masked, 2 * g + 1)
                    scores(b, u, 1)

            run(pe, slot)

        @block.scalar
        def _(act):
            def split_hi(n):
                hi, _, factor = parts_of(n)
                act.wait_ge(s_stage_in[n % 3], 16 * (n // 3 + 1))
                if factor is None:
                    act.activation(hi, stage_of(n), ACT.Copy).then_inc(s_w_hi, 1)
                else:
                    act.activation(hi, stage_of(n), ACT.Copy, scale=factor).then_inc(s_w_hi, 1)

            def x_hi(b, t, bank):
                when(act, s_xt_mm, TT * b + t + 1)
                act.activation(xt_hi[:, b % 2, :, t * P:(t + 1) * P],
                               ps[:, bank, :].rearrange("p (c n) -> p c n", c=DC), ACT.Copy).then_inc(s_xt_hi, 1)

            act.dma_start(gates[:, 0:1], g_xattn.partition_broadcast(P)).then_inc(s_const_in, 16)
            act.dma_start(gates[:, 1:2], g_ffn.partition_broadcast(P)).then_inc(s_const_in, 16)
            act.dma_start(route[:, 0, :], ffn_logits.rearrange("(a e) -> a e", a=1)).then_inc(s_route_in, 16)
            act.dma_start(route[:, 1, :], ffn_u.rearrange("(a e) -> a e", a=1)).then_inc(s_route_in, 16)
            for e in range(2):
                act.dma_start(null_k[DH * e:DH * (e + 1), :], null_kv[0].rearrange("(d o) -> d o", o=1))\
                    .then_inc(s_null_in, 16)
            act.dma_start(v_sb[J:JN, :].rearrange("a (h d) -> a h d", d=DH),
                          null_kv[1:2, :].rearrange("a (h d) -> a h d", h=1).to_broadcast([1, INNER // DH, DH]))\
                .then_inc(s_null_v, 16)
            act.dma_start(mask_u8[:], mask.rearrange("b j -> (b j)").partition_broadcast(P)).then_inc(s_mask, 16)
            act.dma_start(gout[:], g_out.partition_broadcast(P)).then_inc(s_gout, 16)
            act.wait_ge(s_ctx_in, 16)
            act.activation(ctx_hi[:], ctx_in[:], ACT.Copy).then_inc(s_ctx_hi, 1)
            for n in range(CC):
                split_hi(n)
            act.wait_ge(s_route_in, 32)
            act.activation(route[:, 2, :], route[:, 1, :], ACT.Ln).then_inc(s_ra, 1)
            act.wait_ge(s_ra, 1)
            act.activation(route[:, 3, :], route[:, 2, :], ACT.Ln, scale=-1.0).then_inc(s_ra, 1)
            act.wait_ge(s_rd, 1)
            act.activation(route[:, 4, :], route[:, 0, :], ACT.Exp, bias=route[:, 8, 0:1],
                           accum_out=route[:, 9, 0:1]).then_inc(s_ra, 1)
            act.wait_ge(s_ra, 3)
            act.activation(route[:, 9, 1:2], route[:, 9, 0:1], ACT.Ln).then_inc(s_ra, 1)
            act.wait_ge(s_const_in, 48)
            act.activation(tanh_g[:], gates[:], ACT.Tanh).then_inc(s_tanh, 1)
            for n in range(CC, 2 * CC):
                split_hi(n)
            splits = {3: W_Q, 6: W_Q + 1, 9: W_Q + 2, 12: W_Q + 3}
            for j in range(2 * NU):
                c, h = j // 2, j % 2
                if c >= 2:
                    act.wait_ge(s_k_out[c % 2], 32 * (c // 2))
                act.wait_ge(s_k_mm, j + 1)
                act.activation(k_st[:, c % 2, 0, h * JH:(h + 1) * JH], ps[:, j % 8, 0:JH], ACT.Copy,
                               scale=DH ** -0.5).then_inc(s_k_hi, 1)
                if j in splits:
                    split_hi(splits[j])
            for t in range(TT):
                x_hi(0, t, t)
            for m in range(VT):
                rows = min(P, BJ - m * P)
                if m >= 2:
                    act.wait_ge(s_v_out[m % 2], 16 * (m // 2))
                act.wait_ge(s_v_mm, 2 * m + 1)
                act.activation(v_st[0:rows, m % 2, 0:512], ps[0:rows, (4 + 2 * m) % 8, :], ACT.Copy)\
                    .then_inc(s_v_act, 1)
            act.wait_ge(s_kz, 2)
            act.wait_ge(s_null_in, 32)
            for e in range(2):
                rows = slice(DH * e, DH * (e + 1))
                act.activation(k_bd[rows, 0, :, JN * e + J], null_k[rows, 0:1].to_broadcast([DH, NU]), ACT.Copy,
                               scale=DH ** -0.5).then_inc(s_null_hi, 1)

            def norm_z(b, t):
                when(act, s_z_nmr, TT * (b - 1) + t + 1)
                act.activation(zn[:, t % 2, :], row[:, t, :], ACT.Identity, bias=z_nmr[:, t:t + 1],
                               scale=z_rstd[:, t:t + 1]).then_inc(s_zn, 1)

            def z_hi(b, t, bank):
                when(act, s_zt_mm, TT * (b - 1) + t + 1)
                if t >= 2:
                    when(act, s_f_mm, TT * (b - 1) + t - 1)
                act.activation(zt_hi[:, t % 2, :, :], ps[:, bank, :].rearrange("p (c n) -> p c n", c=DC),
                               ACT.Copy).then_inc(s_zt_hi, 1)

            def slot(b, u):
                cur, nxt, prev = has(b)
                g = b * NU + u
                sv, _ = unit_back(b, u, 1)
                pv, _ = unit_back(b, u, 2)
                if prev and u == 3:
                    when(act, s_res_in, 16 * b)
                    when(act, s_y_nmr, b)
                    for t in range(TT):
                        act.activation(row[:, t, :], ps[:, t, :], ACT.Identity, bias=y_nmr[:, t:t + 1],
                                       scale=y_rstd[:, t:t + 1]).then_inc(s_yn, 1)
                if cur:
                    when(act, s_s_mm, 2 * g)
                    when(act, s_q_mm, g + 1)
                    act.activation(q_hi[:], ps[:, WORK, :], ACT.Copy).then_inc(s_q_hi, 1)
                if pv:
                    when(act, s_pv_mm, g - 2)
                    for e in range(2):
                        when(act, s_pt_mm, 2 * (g - 2) + e + 1)
                        act.activation(p_t[:, e, :], ps[0:JN, WORK + 1 + e, :], ACT.Copy).then_inc(s_pt, 1)
                if sv:
                    when(act, s_sub, g)
                    i = (u - 1) % 2
                    act.activation(prob[:, i, :, :], prob[:, i, :, :], ACT.Exp).then_inc(s_exp, 1)
                for n in splits_in(b, u):
                    if n == W_O:
                        act.wait_ge(s_v_mm, 2 * VT)
                    split_hi(n)
                if prev:
                    for t in {4: [0], 5: [1], 6: [3]}.get(u, []):
                        norm_z(b, t)
                if pv:
                    when(act, s_y_mm, TT * (g - 2))
                    when(act, s_pv_mm, g - 1)
                    act.activation(o_hi[:], ps[:, WORK + 1, :], ACT.Copy).then_inc(s_o_hi, 1)
                if nxt and 1 <= u < TT:
                    x_hi(b + 1, u - 1, WORK + 2)
                if prev:
                    if u == 4:
                        z_hi(b, 0, WORK)
                    if u == 5:
                        norm_z(b, 2)
                        z_hi(b, 1, WORK + 2)
                        z_hi(b, 2, WORK + 2)
                    if u == 6:
                        z_hi(b, 3, WORK + 2)
                if nxt and u == TT:
                    x_hi(b + 1, u - 1, WORK + 2)

            run(act, slot)

        @block.vector
        def _(dve):
            def split_lo(n):
                hi, lo, factor = parts_of(n)
                dve.wait_ge(s_w_hi, n + 1)
                if factor is None:
                    dve.tensor_tensor(lo, stage_of(n), hi.bitcast(F32), ALU.subtract).then_inc(s_w_lo, 1)
                else:
                    dve.scalar_tensor_tensor(out=lo, in0=stage_of(n), scalar=factor, in1=hi.bitcast(F32),
                                             op0=ALU.mult, op1=ALU.subtract).then_inc(s_w_lo, 1)

            def after(semaphore, count):
                if not isinstance(count, int):
                    count = dve.snap(dve.to_reg(count))
                    dve.wait_ge(s_ctx_lo, 1)
                dve.wait_ge(semaphore, count)

            def x_stats(b, t):
                dve.wait_ge(s_x_in[t], 16 * (b + 1))
                dve.bn_stats(x_stat[:, t, :], xin[:, t, :]).then_inc(s_x_bn, 1)
                after(s_x_bn, TT * b + t + 1)
                dve.bn_aggr(x_mv[:, t, :], x_stat[:, t, :]).then_inc(s_x_mv, 1)
                dve.wait_ge(s_x_mv, TT * b + t + 1)
                dve.tensor_scalar(x_var[:, t:t + 1], x_mv[:, t, 1:2], 1.0 + EPS, EPS * EPS,
                                  ALU.mult, ALU.add).then_inc(s_x_var, 1)

            def x_norm(b, t):
                when(dve, s_x_rstd, TT * b + t + 1)
                dve.tensor_scalar(xin[:, t, :], xin[:, t, :], x_mv[:, t, 0:1], x_rstd[:, t:t + 1],
                                  ALU.subtract, ALU.mult).then_inc(s_xn, 1)

            def x_lo(b, t, bank):
                when(dve, s_xt_hi, TT * b + t + 1)
                cols = slice(t * P, (t + 1) * P)
                dve.tensor_tensor(xt_lo[:, b % 2, :, cols], ps[:, bank, :].rearrange("p (c n) -> p c n", c=DC),
                                  xt_hi[:, b % 2, :, cols].bitcast(F32), ALU.subtract).then_inc(s_xt_lo, 1)

            dve.memset(k_bd[:, 0].bitcast(F32), 0.0).then_inc(s_kz, 1)
            dve.memset(k_bd[:, 1].bitcast(F32), 0.0).then_inc(s_kz, 1)
            dve.wait_ge(s_route_in, 32)
            dve.tensor_reduce(route[:, 8, 0:1], route[:, 0, :], AX.X, ALU.max, negate=True).then_inc(s_rd, 1)
            dve.wait_ge(s_ctx_hi, 1)
            dve.tensor_tensor(ctx_lo[:], ctx_in[:], ctx_hi[:].bitcast(F32), ALU.subtract).then_inc(s_ctx_lo, 1)
            for n in range(CC):
                split_lo(n)
            dve.memset(mask_bias[:], 0.0).then_inc(s_rd, 1)
            dve.wait_ge(s_ra, 4)
            dve.wait_ge(s_rd, 2)
            dve.tensor_scalar(route[:, 5, :], route[:, 0, :], route[:, 8, 0:1], route[:, 9, 1:2],
                              ALU.add, ALU.subtract).then_inc(s_rd, 1)
            dve.wait_ge(s_mask, 16)
            dve.tensor_scalar(mask_bias[:, :, 0:J], mask_u8[:].rearrange("p (b j) -> p b j", b=B), 1.0, MASKED,
                              ALU.subtract, ALU.mult).then_inc(s_mask, 1)
            dve.wait_ge(s_rd, 3)
            dve.tensor_tensor(route[:, 6, :], route[:, 5, :], route[:, 3, :], ALU.subtract).then_inc(s_rd, 1)
            dve.wait_ge(s_rd, 4)
            dve.max(route[:, 7, :], route[:, 6, :]).then_inc(s_rd, 1)
            dve.wait_ge(s_rd, 5)
            dve.max_index(route_i[:], route[:, 7, :], route[:, 6, :]).then_inc(s_expert, 1)
            for n in range(CC, 2 * CC):
                split_lo(n)
            splits = {3: W_Q, 6: W_Q + 1, 9: W_Q + 2, 12: W_Q + 3}
            for j in range(2 * NU):
                c, h = j // 2, j % 2
                dve.wait_ge(s_k_hi, j + 1)
                toks = slice(h * JH, (h + 1) * JH)
                dve.scalar_tensor_tensor(out=k_st[:, c % 2, 1, toks], in0=ps[:, j % 8, 0:JH], scalar=DH ** -0.5,
                                         in1=k_st[:, c % 2, 0, toks].bitcast(F32), op0=ALU.mult,
                                         op1=ALU.subtract).then_inc(s_k_lo, 1)
                if j in splits:
                    split_lo(splits[j])
                if j % 4 == 1:
                    x_stats(0, j // 4)
                if j % 4 == 3:
                    x_norm(0, j // 4)
            for t in range(TT):
                x_lo(0, t, t)
            for m in range(VT):
                rows = min(P, BJ - m * P)
                if m >= 2:
                    dve.wait_ge(s_v_out[m % 2], 16 * (m // 2))
                dve.wait_ge(s_v_mm, 2 * m + 2)
                dve.tensor_copy(v_st[0:rows, m % 2, 512:1024], ps[0:rows, (5 + 2 * m) % 8, :]).then_inc(s_v_dve, 1)
            dve.wait_ge(s_null_hi, 2)
            for e in range(2):
                rows = slice(DH * e, DH * (e + 1))
                nl = dve.scalar_tensor_tensor(out=k_bd[rows, 1, :, JN * e + J], in0=null_k[rows, 0:1].to_broadcast([DH, NU]),
                                              scalar=DH ** -0.5, in1=k_bd[rows, 0, :, JN * e + J].bitcast(F32),
                                              op0=ALU.mult, op1=ALU.subtract)
            nl.then_inc(s_null, 1)
            dve.wait_ge(s_gout, 16)
            dve.wait_ge(s_tanh, 1)
            dve.tensor_scalar(gout[:], gout[:], tanh_g[:, 0:1], None, ALU.mult).then_inc(s_gout, 1)

            def y_stats(b):
                for t in range(TT):
                    when(dve, s_y_mm, TT * (b * NU - 1) + t + 1)
                    dve.bn_stats(y_stat[:, t, :], ps[:, t, :]).then_inc(s_y_bn, 1)
                after(s_y_bn, TT * b)
                for t in range(TT):
                    dve.bn_aggr(y_mv[:, t, :], y_stat[:, t, :]).then_inc(s_y_mv, 1)
                dve.wait_ge(s_y_mv, TT * b)
                dve.tensor_scalar(y_var[:], y_mv[:, :, 1], EPS, None, ALU.add).then_inc(s_y_var, 1)

            def x1_stats(b, t):
                when(dve, s_yg, TT * (b - 1) + t + 1)
                dve.tensor_tensor(row[:, t, :], row[:, t, :], x_res[:, t, :], ALU.add).then_inc(s_x1, 1)
                dve.wait_ge(s_x1, TT * (b - 1) + t + 1)
                dve.bn_stats(z_stat[:, t, :], row[:, t, :]).then_inc(s_z_bn, 1)
                after(s_z_bn, TT * (b - 1) + t + 1)
                dve.bn_aggr(z_mv[:, t, :], z_stat[:, t, :]).then_inc(s_z_mv, 1)
                dve.wait_ge(s_z_mv, TT * (b - 1) + t + 1)
                dve.tensor_scalar(z_var[:, t:t + 1], z_mv[:, t, 1:2], EPS, None, ALU.add).then_inc(s_z_var, 1)

            def z_shift(b, t):
                when(dve, s_z_rstd, TT * (b - 1) + t + 1)
                dve.scalar_tensor_tensor(out=z_nmr[:, t:t + 1], in0=z_mv[:, t, 0:1], scalar=-1.0,
                                         in1=z_rstd[:, t:t + 1], op0=ALU.mult, op1=ALU.mult).then_inc(s_z_nmr, 1)

            def z_lo(b, t, bank):
                when(dve, s_zt_hi, TT * (b - 1) + t + 1)
                dve.tensor_tensor(zt_lo[:, t % 2, :, :], ps[:, bank, :].rearrange("p (c n) -> p c n", c=DC),
                                  zt_hi[:, t % 2, :, :].bitcast(F32), ALU.subtract).then_inc(s_zt_lo, 1)

            def result(b, t, bank):
                when(dve, s_x1b, TT * (b - 1) + t + 1)
                when(dve, s_f_mm, TT * (b - 1) + t + 1)
                dve.tensor_tensor(row[:, t, :], ps[:, bank, :], row[:, t, :], ALU.add).then_inc(s_res, 1)

            def unmask(b, u, half):
                when(dve, s_s_mm, 2 * (b * NU + u) + half + 1)
                dve.tensor_tensor(prob[:, u % 2, 4 * half:4 * half + 4, :], psum_scores,
                                  mask_bias[:, bass.ds(b, 1), :].to_broadcast([P, 4, JN]),
                                  ALU.add).then_inc(s_masked, 1)

            def slot(b, u):
                cur, nxt, prev = has(b)
                g = b * NU + u
                sv, _ = unit_back(b, u, 1)
                pv, _ = unit_back(b, u, 2)
                if cur:
                    when(dve, s_q_hi, g + 1)
                    dve.tensor_tensor(q_lo[:], ps[:, WORK, :], q_hi[:].bitcast(F32), ALU.subtract)\
                        .then_inc(s_q_lo, 1)
                if prev:
                    for t in {4: [0], 5: [1, 2], 6: [3]}.get(u, []):
                        z_shift(b, t)
                if nxt and 1 <= u <= TT:
                    x_norm(b + 1, u - 1)
                for n in splits_in(b, u):
                    split_lo(n)
                if isinstance(b, int) and b == 0 and u == 5:
                    dve.wait_ge(s_bias_in, 16)
                    dve.tensor_scalar(bias[:], bias[:], tanh_g[:, 1:2], None, ALU.mult).then_inc(s_bias, 1)
                if prev:
                    for t in {4: [1], 5: [3]}.get(u, []):
                        x1_stats(b, t)
                if sv:
                    when(dve, s_exp, g)
                    dve.tensor_reduce(s_sum[:], prob[:, (u - 1) % 2, :, :], AX.X, ALU.add).then_inc(s_sum_ok, 1)
                    when(dve, s_sum_ok, g)
                    when(dve, s_prob, g - 1)
                    dve.reciprocal(s_rcp[:], s_sum[:]).then_inc(s_rcp_ok, 1)
                if prev and u == 2:
                    y_stats(b)
                if cur:
                    if u == 0 and isinstance(b, int) and b == 0:
                        dve.wait_ge(s_mask, 17)
                    when(dve, s_pt_mm, 2 * (g - 1))
                    unmask(b, u, 0)
                if prev and u == 2:
                    when(dve, s_y_rstd, b)
                    dve.scalar_tensor_tensor(out=y_nmr[:], in0=y_mv[:, :, 0], scalar=-1.0, in1=y_rstd[:],
                                             op0=ALU.mult, op1=ALU.mult).then_inc(s_y_nmr, 1)
                if pv:
                    when(dve, s_o_hi, g - 1)
                    dve.tensor_tensor(o_lo[:], ps[:, WORK + 1, :], o_hi[:].bitcast(F32), ALU.subtract)\
                        .then_inc(s_o_lo, 1)
                if nxt and 1 <= u < TT:
                    x_lo(b + 1, u - 1, WORK + 2)
                if prev:
                    if u == 4:
                        z_lo(b, 0, WORK)
                    if u == 5:
                        z_lo(b, 1, WORK + 2)
                        result(b, 0, WORK)
                        z_lo(b, 2, WORK + 2)
                    if u == 6:
                        result(b, 1, WORK)
                        z_lo(b, 3, WORK + 2)
                    if u == 7:
                        result(b, 2, WORK + 2)
                        result(b, 3, WORK + 1)
                if nxt and u == TT:
                    x_lo(b + 1, u - 1, WORK + 2)
                if cur:
                    unmask(b, u, 1)
                    when(dve, s_masked, 2 * g + 2)
                    dve.tensor_reduce(s_top[:], prob[:, u % 2, :, :], AX.X, ALU.max).then_inc(s_top_ok, 1)
                if nxt and u < TT:
                    x_stats(b + 1, u)
                if prev:
                    for t in {3: [0], 4: [2]}.get(u, []):
                        x1_stats(b, t)

            run(dve, slot)

        @block.gpsimd
        def _(pool):
            def spread(ap):
                return ap.rearrange("p (g o) -> p g o", o=1).to_broadcast([P, 2 * TT, JN])

            def x_power(b, t):
                when(pool, s_x_var, TT * b + t + 1)
                pool.tensor_tensor(x_rstd[:, t:t + 1], x_var[:, t:t + 1], half_neg[:, 0:1], ALU.pow)\
                    .then_inc(s_x_rstd, 1)
            def z_power(b, t):
                when(pool, s_z_var, TT * (b - 1) + t + 1)
                pool.tensor_tensor(z_rstd[:, t:t + 1], z_var[:, t:t + 1], half_neg[:, 0:1], ALU.pow)\
                    .then_inc(s_z_rstd, 1)

            def add_bias(b, t):
                when(pool, s_zn, TT * (b - 1) + t + 1)
                pool.tensor_tensor(row[:, t, :], row[:, t, :], bias[:], ALU.add).then_inc(s_x1b, 1)

            pool.memset(half_neg[:], -0.5)
            pool.memset(ident[:], 0.0).then_inc(s_ident, 1)
            pool.wait_ge(s_ident, 1)
            pool.affine_select(out=ident[:], in_=ident[:], compare_op=ALU.not_equal, fill=1.0, base=0,
                               pattern=[[-1, P]], channel_multiplier=1).then_inc(s_ident, 1)
            for t in range(TT):
                x_power(0, t)

            def slot(b, u):
                cur, nxt, prev = has(b)
                g = b * NU + u
                sv, _ = unit_back(b, u, 1)
                i = (u - 1) % 2
                if nxt and 1 <= u <= TT:
                    x_power(b + 1, u - 1)
                if sv:
                    when(pool, s_top_ok, g)
                    pool.tensor_tensor(prob[:, i, :, :], prob[:, i, :, :], spread(s_top[:]), ALU.subtract)\
                        .then_inc(s_sub, 1)

                def gains(t):
                    when(pool, s_yn, TT * (b - 1) + t + 1)
                    pool.tensor_tensor(row[:, t, :], row[:, t, :], gout[:], ALU.mult).then_inc(s_yg, 1)

                if prev and u == 3:
                    if not isinstance(b, int) or b == 1:
                        pool.wait_ge(s_gout, 17)
                    gains(0)
                    gains(1)
                if prev:
                    for t in {4: [0], 5: [2]}.get(u, []):
                        z_power(b, t)
                if sv:
                    when(pool, s_rcp_ok, g)
                    pool.tensor_tensor(prob[:, i, :, :], prob[:, i, :, :], spread(s_rcp[:]), ALU.mult)\
                        .then_inc(s_prob, 1)
                if prev:
                    if u == 2:
                        when(pool, s_y_var, b)
                        pool.tensor_tensor(y_rstd[:], y_var[:], half_neg[:], ALU.pow).then_inc(s_y_rstd, 1)
                    if u == 3:
                        for t in range(2, TT):
                            gains(t)
                    if u == 4 and (not isinstance(b, int) or b == 1):
                        pool.wait_ge(s_bias, 1)
                    for t in {4: [1], 5: [3]}.get(u, []):
                        z_power(b, t)
                    for t in {4: [0], 5: [1, 2], 6: [3]}.get(u, []):
                        add_bias(b, t)

            run(pool, slot)


_INS = ["x", "ctx_768", "mask_BxS2_bf1", "g_xattn", "g_ffn", "L0_xattn_g_norm", "L0_xattn_null_kv", "L0_xattn_Wq",
        "L0_xattn_Wkv", "L0_xattn_Wout", "L0_xattn_g_out", "L0_ffn_W", "L0_ffn_b", "L0_ffn_logits", "L0_ffn_u"]


def kernel(**inputs):
    import numpy as np
    import concourse.bacc as bacc
    from concourse import mybir as mb
    from concourse.bass_utils import run_bass_kernel_spmd

    nc = bacc.Bacc("TRN2", target_bir_lowering=False, num_devices=1)
    arrays, args = {}, []
    for name in _INS:
        a = np.asarray(inputs[name])
        if name == "ctx_768":
            a = a.reshape(-1, a.shape[-1]).T
        if name == "L0_xattn_g_norm":
            a = a.reshape(-1, P).T
        a = np.ascontiguousarray(a)
        if a.dtype == np.bool_:
            a = a.view(np.uint8)
        arrays[f"in_{name}"] = a
        args.append(nc.dram_tensor(f"in_{name}", a.shape, mb.dt.from_np(a.dtype), kind="ExternalInput").ap())
    shape = inputs["x"].shape
    args.append(nc.dram_tensor("out_0", shape, mb.dt.float32, kind="ExternalOutput").ap())
    flamingo_program(nc, *args)
    r = run_bass_kernel_spmd(nc, [arrays], core_ids=[0])
    return r.results[0]["out_0"]
```

```python
from contextlib import ExitStack

import concourse.bass as bass
from concourse import mybir

F32 = mybir.dt.float32
F32R = mybir.dt.float32r
U32 = mybir.dt.uint32
U8 = mybir.dt.uint8
ALU = mybir.AluOpType
ACT = mybir.ActivationFunctionType
AX = mybir.AxisListType

P = 128
EPS = 1e-5
MASKED = 3.0e38
DH = 64


def flamingo_program(nc, x, ctx_t, mask, g_xattn, g_ffn, g_norm, null_kv, w_q, w_kv, w_out, g_out,
                     ffn_w, ffn_b, ffn_logits, ffn_u, out):
    B, N, D = x.shape
    C, BJ = ctx_t.shape
    J = BJ // B
    JN = J + 1
    INNER = w_q.shape[1]
    E = ffn_w.shape[0]
    TT = N // P
    DC = D // P
    CC = C // P
    NU = INNER // P
    HALF = NU // 2
    W2 = 2 * JN
    JH = BJ // 2
    VT = (BJ + P - 1) // P
    assert (TT, DC, NU) == (4, 4, 8) and N == 512 and D == 512 and BJ % 2 == 0

    x_tok = x.rearrange("b n d -> (b n) d")
    out_tok = out.rearrange("b n d -> (b n) d")

    stack = ExitStack()

    def sb(name, shape, dt=F32):
        return stack.enter_context(nc.sbuf_tensor(name, shape, dt))

    def sem(name):
        return stack.enter_context(nc.semaphore(name))

    k_dram = nc.dram_tensor("k_dram", (2, INNER, BJ), F32, kind="Internal").ap()
    v_dram = nc.dram_tensor("v_dram", (BJ, INNER), F32, kind="Internal").ap()

    with stack:
        ps = stack.enter_context(nc.psum_tensor("ps", [P, 8, 512], F32))
        SCORE, WORK = 4, 5

        wq_hi = sb("wq_hi", [P, DC, INNER], F32R)
        wq_lo = sb("wq_lo", [P, DC, INNER], F32R)
        xt_hi = sb("xt_hi", [P, 2, DC, N], F32R)
        xt_lo = sb("xt_lo", [P, 2, DC, N], F32R)
        k_bd = sb("k_bd", [P, 2, NU, W2], F32R)
        v_sb = sb("v_sb", [JN, INNER])
        xin = sb("xin", [P, TT, D])
        stage = sb("stage", [P, 3, 1024])
        gout = sb("gout", [P, D])
        bias = sb("bias", [P, D])
        mask_bias = sb("mask_bias", [P, B, JN])
        ident = sb("ident", [P, P])
        gn = sb("gn", [P, DC])
        half_neg = sb("half_neg", [P, TT])
        gates = sb("gates", [P, 2])
        tanh_g = sb("tanh_g", [P, 2])
        null_k = sb("null_k", [P, 1])
        route = sb("route", [1, 10, 8])
        route_i = sb("route_i", [1, 8], U32)
        x_stat = sb("x_stat", [P, TT, 6])
        x_mv = sb("x_mv", [P, TT, 2])
        x_var = sb("x_var", [P, TT])
        x_rstd = sb("x_rstd", [P, TT])
        y_stat = sb("y_stat", [P, TT, 6])
        y_mv = sb("y_mv", [P, TT, 2])
        y_var = sb("y_var", [P, TT])
        y_rstd = sb("y_rstd", [P, TT])
        z_stat = sb("z_stat", [P, TT, 6])
        z_mv = sb("z_mv", [P, TT, 2])
        z_var = sb("z_var", [P, TT])
        z_rstd = sb("z_rstd", [P, TT])
        z_nmr = sb("z_nmr", [P, TT])
        s_top = sb("s_top", [P, 2 * TT])
        s_sum = sb("s_sum", [P, 2 * TT])
        s_rcp = sb("s_rcp", [P, 2 * TT])

        early = ExitStack()
        with early:
            def esb(name, shape, dt=F32):
                return early.enter_context(nc.sbuf_tensor(name, shape, dt))
            wkv_hi = esb("wkv_hi", [P, 2, CC, INNER], F32R)
            wkv_lo = esb("wkv_lo", [P, 2, CC, INNER], F32R)
            ctx_hi = esb("ctx_hi", [P, CC, BJ], F32R)
            ctx_lo = esb("ctx_lo", [P, CC, BJ], F32R)
            ctx_in = esb("ctx_in", [P, CC, BJ])
            k_st = esb("k_st", [P, 2, 2, BJ], F32R)
            v_st = esb("v_st", [P, 2, INNER])
        wo_hi = sb("wo_hi", [P, NU, D], F32R)
        wo_lo = sb("wo_lo", [P, NU, D], F32R)
        wf_hi = sb("wf_hi", [P, DC, D], F32R)
        wf_lo = sb("wf_lo", [P, DC, D], F32R)
        p_t = sb("p_t", [JN, 2, N])
        o_hi = sb("o_hi", [P, N], F32R)
        o_lo = sb("o_lo", [P, N], F32R)
        prob = sb("prob", [P, 2, 2 * TT, JN])
        q_hi = sb("q_hi", [P, N], F32R)
        q_lo = sb("q_lo", [P, N], F32R)
        zn = sb("zn", [P, 2, D])
        zt_hi = sb("zt_hi", [P, 2, DC, P], F32R)
        zt_lo = sb("zt_lo", [P, 2, DC, P], F32R)
        row = sb("row", [P, TT, D])
        x_res = sb("x_res", [P, TT, D])
        mask_u8 = sb("mask_u8", [P, B * J], U8)

        s_ctx_in = [sem(f"s_ctx_in{c}") for c in range(CC)]
        s_gn_in = sem("s_gn_in")
        s_const_in = sem("s_const_in")
        s_route_in = sem("s_route_in")
        s_stage_in = [sem(f"s_stage_in{i}") for i in range(3)]
        s_x_in = [sem(f"s_x_in{t}") for t in range(TT)]
        s_res_in = sem("s_res_in")
        s_bias_in = sem("s_bias_in")
        s_k_in = [sem(f"s_k_in{h}") for h in range(2)]
        s_v_in = [sem(f"s_v_in{h}") for h in range(2)]
        s_k_out = [sem(f"s_k_out{i}") for i in range(2)]
        s_v_out = [sem(f"s_v_out{i}") for i in range(2)]
        s_null_in = sem("s_null_in")
        s_null_v = sem("s_null_v")
        s_mask_in = sem("s_mask_in")
        s_gout_in = sem("s_gout_in")
        s_out = sem("s_out")
        s_ident = sem("s_ident")
        s_tanh = sem("s_tanh")
        s_ra = sem("s_ra")
        s_rd = sem("s_rd")
        s_expert = sem("s_expert")
        s_ctx_hi = sem("s_ctx_hi")
        s_ctx_lo = sem("s_ctx_lo")
        s_w_hi = sem("s_w_hi")
        s_w_lo = sem("s_w_lo")
        s_k_mm = sem("s_k_mm")
        s_k_hi = sem("s_k_hi")
        s_k_lo = sem("s_k_lo")
        s_v_mm = sem("s_v_mm")
        s_v_act = sem("s_v_act")
        s_v_dve = sem("s_v_dve")
        s_kz = sem("s_kz")
        s_null_hi = sem("s_null_hi")
        s_null = sem("s_null")
        s_mask = sem("s_mask")
        s_bias = sem("s_bias")
        s_q_mm = sem("s_q_mm")
        s_s_mm = sem("s_s_mm")
        s_pt_mm = sem("s_pt_mm")
        s_pv_mm = sem("s_pv_mm")
        s_y_mm = sem("s_y_mm")
        s_xt_mm = sem("s_xt_mm")
        s_zt_mm = sem("s_zt_mm")
        s_f_mm = sem("s_f_mm")
        s_q_hi = sem("s_q_hi")
        s_exp = sem("s_exp")
        s_pt = sem("s_pt")
        s_o_hi = sem("s_o_hi")
        s_xt_hi = sem("s_xt_hi")
        s_y = sem("s_y")
        s_zn = sem("s_zn")
        s_zt_hi = sem("s_zt_hi")
        s_q_lo = sem("s_q_lo")
        s_masked = sem("s_masked")
        s_top_ok = sem("s_top_ok")
        s_sum_ok = sem("s_sum_ok")
        s_rcp_ok = sem("s_rcp_ok")
        s_o_lo = sem("s_o_lo")
        s_xt_lo = sem("s_xt_lo")
        s_x_bn = sem("s_x_bn")
        s_x_mv = sem("s_x_mv")
        s_x_var = sem("s_x_var")
        s_y_bn = sem("s_y_bn")
        s_y_mv = sem("s_y_mv")
        s_y_var = sem("s_y_var")
        s_yg = sem("s_yg")
        s_x1 = sem("s_x1")
        s_z_bn = sem("s_z_bn")
        s_z_mv = sem("s_z_mv")
        s_z_var = sem("s_z_var")
        s_z_nmr = sem("s_z_nmr")
        s_zt_lo = sem("s_zt_lo")
        s_res = sem("s_res")
        s_sub = sem("s_sub")
        s_prob = sem("s_prob")
        s_x_rstd = sem("s_x_rstd")
        s_xn = sem("s_xn")
        s_y_rstd = sem("s_y_rstd")
        s_z_rstd = sem("s_z_rstd")
        s_x1b = sem("s_x1b")

        chunks = [w_kv[c * P:(c + 1) * P, h * INNER:(h + 1) * INNER] for h in range(2) for c in range(CC)]
        chunks += [w_q[c * P:(c + 1) * P, :] for c in range(DC)]
        chunks += [w_out[2 * c * P:2 * (c + 1) * P, :].rearrange("(a p) d -> p a d", p=P) for c in range(NU // 2)]
        W_K, W_V, W_Q, W_O = 0, CC, 2 * CC, 2 * CC + DC
        W_F = W_O + NU // 2
        W_END = W_F + DC // 2

        def stage_of(n):
            s = stage[:, n % 3, :]
            return s if n < W_O else s.rearrange("p (a d) -> p a d", a=2)

        def parts_of(n):
            if n < W_Q:
                return wkv_hi[:, n // CC, n % CC, :], wkv_lo[:, n // CC, n % CC, :], None
            if n < W_O:
                c = n - W_Q
                return wq_hi[:, c, :], wq_lo[:, c, :], gn[:, c:c + 1]
            if n < W_F:
                c = 2 * (n - W_O)
                return wo_hi[:, c:c + 2, :], wo_lo[:, c:c + 2, :], None
            c = 2 * (n - W_F)
            return wf_hi[:, c:c + 2, :], wf_lo[:, c:c + 2, :], tanh_g[:, 1:2]

        EARLY_V = 2
        KEY_SPLITS = {7: CC + 2, 11: W_Q}
        RING_SPLITS = {0: W_Q + 1, 2: W_Q + 2, 6: W_Q + 3}

        def when(engine, semaphore, count):
            if not isinstance(count, int) or count > 0:
                engine.wait_ge(semaphore, count)

        def splits_in(b, u):
            if isinstance(b, int) and b == 0:
                return {0: [W_O], 2: [W_O + 1], 3: [W_O + 2], 4: [W_O + 3], 5: [W_F], 6: [W_F + 1]}.get(u, [])
            return []

        def run(engine, slot):
            for u in range(NU):
                slot(0, u)
            with engine.Fori(1, B - 1) as b:
                for u in range(NU):
                    slot(b, u)
            for u in range(NU):
                slot(B - 1, u)
            for u in range(3):
                slot(B, u)

        def has(b):
            if isinstance(b, int):
                return b < B, b + 1 < B, 0 < b < B
            return True, True, True

        def unit_back(b, u, lag):
            there = not isinstance(b, int) or 0 <= NU * b + u - lag < NU * B
            return there, (u - lag) % NU

        X_STATS_A, X_STATS_B = {0: [0], 1: [2]}, {0: [1], 1: [3]}
        X_NORM_A, X_NORM_B = {1: [0], 2: [2, 3]}, {1: [1]}
        X_TURN_5, X_TURN_7 = {1: [0], 3: [3]}, {1: [1], 2: [2]}

        ring = [("v", n) for n in range(4)]
        for t in range(TT):
            ring += [("x", t), ("v", 4 + t)]
        ring += [("v", n) for n in range(8, 2 * VT)]

        psum_scores = ps[:, SCORE, 0:2 * W2].rearrange("p (g j) -> p g j", j=JN)

        block = stack.enter_context(nc.Block())

        @block.sync
        def _(sp):
            def load_stage(n, src):
                if n >= 3:
                    sp.wait_ge(s_w_lo, n - 2)
                sp.dma_start(stage_of(n), src).then_inc(s_stage_in[n % 3], 16)

            def load_keys(b, h):
                for part in range(2):
                    for e in range(2):
                        src = k_dram[part, h * HALF * P:(h + 1) * HALF * P, bass.ds(b * J, J)]
                        src = src.rearrange("(u e d) j -> e d u j", u=HALF, e=2)[e]
                        dst = k_bd[DH * e:DH * (e + 1), part, h * HALF:(h + 1) * HALF, JN * e:JN * e + J]
                        sp.dma_start(dst.bitcast(F32), src).then_inc(s_k_in[h], 16)

            def load_values(b, h):
                cols = slice(h * HALF * P, (h + 1) * HALF * P)
                sp.dma_start(v_sb[0:J, cols], v_dram[bass.ds(b * J, J), cols]).then_inc(s_v_in[h], 16)

            def load_x(b, t):
                sp.dma_start(xin[:, t, :], x_tok[bass.ds(b * N + t * P, P), :]).then_inc(s_x_in[t], 16)

            for c in range(CC):
                sp.dma_start(ctx_in[:, c, :], ctx_t[c * P:(c + 1) * P, :]).then_inc(s_ctx_in[c], 16)
                load_stage(c, chunks[c])
            sp.dma_start(gn[:], g_norm).then_inc(s_gn_in, 16)
            for n in range(CC, W_Q):
                load_stage(n, chunks[n])
            for t in range(TT):
                load_x(0, t)
            for c in range(NU):
                sp.wait_ge(s_k_lo, 2 * (c + 1))
                for part in range(2):
                    sp.dma_start(k_dram[part, c * P:(c + 1) * P, :], k_st[:, c % 2, part, :].bitcast(F32))\
                        .then_inc(s_k_out[c % 2], 16)
                if c < 3:
                    load_stage(W_Q + c, chunks[W_Q + c])
            sp.wait_ge(s_kz, 2)
            for i in range(2):
                sp.wait_ge(s_k_out[i], 32 * (NU // 2))
            for h in range(2):
                load_keys(0, h)
            for m in range(VT):
                if m == 1:
                    for n in range(W_Q + 3, W_O + 2):
                        load_stage(n, chunks[n])
                if m == VT - 1:
                    for t in range(TT):
                        sp.wait_ge(s_xt_mm, t + 1)
                        load_x(1, t)
                rows = min(P, BJ - m * P)
                sp.wait_ge(s_v_act, m + 1)
                sp.wait_ge(s_v_dve, m + 1)
                sp.dma_start(v_dram[m * P:m * P + rows, :], v_st[0:rows, m % 2, :]).then_inc(s_v_out[m % 2], 16)
            sp.wait_ge(s_v_out[0], 16 * ((VT + 1) // 2))
            sp.wait_ge(s_v_out[1], 16 * (VT // 2))
            for h in range(2):
                load_values(0, h)
            sp.wait_ge(s_expert, 1)
            expert = sp.value_load(route_i[0:1, 0:1], min_val=0, max_val=E - 1)
            sp.dma_start(bias[:], ffn_b[bass.ds(expert, 1), :].partition_broadcast(P)
                         .rearrange("p a d -> p (a d)")).then_inc(s_bias_in, 16)
            load_stage(W_O + 2, chunks[W_O + 2])
            load_stage(W_O + 3, chunks[W_O + 3])
            for c in range(DC // 2):
                src = ffn_w[bass.ds(expert, 1), 2 * c * P:2 * (c + 1) * P, :]
                load_stage(W_F + c, src.rearrange("a (c p) d -> p (a c) d", p=P))

            def batch(b):
                cur, nxt, _ = has(b)
                prev = not (isinstance(b, int) and b == 0)
                if cur and prev:
                    when(sp, s_pv_mm, NU * b)
                    load_values(b, 1)
                if nxt:
                    when(sp, s_s_mm, 2 * (NU * b + HALF))
                    load_keys(b + 1, 0)
                    if not (isinstance(b, int) and b + 2 >= B):
                        for t in range(TT):
                            when(sp, s_xt_mm, TT * (b + 1) + t + 1)
                            load_x(b + 2, t)
                    when(sp, s_pv_mm, NU * b + HALF)
                    load_values(b + 1, 0)
                    when(sp, s_s_mm, 2 * (NU * b + NU))
                    load_keys(b + 1, 1)
                if prev:
                    for t in range(TT):
                        when(sp, s_res, TT * (b - 1) + t + 1)
                        sp.dma_start(out_tok[bass.ds((b - 1) * N + t * P, P), :], row[:, t, :])\
                            .then_inc(s_out, 16)
                if cur:
                    if prev:
                        when(sp, s_out, 16 * TT * b)
                    sp.dma_start(x_res[:], x_tok[bass.ds(b * N, N), :].rearrange("(t p) d -> p t d", p=P))\
                        .then_inc(s_res_in, 16)

            batch(0)
            with sp.Fori(1, B - 2) as b:
                batch(b)
            batch(B - 2)
            batch(B - 1)
            batch(B)
            sp.wait_ge(s_out, 16 * TT * B)

        @block.tensor
        def _(pe):
            def three(out_ap, terms, first, last):
                mm = None
                for n, (a_hi, a_lo, b_hi, b_lo) in enumerate(terms):
                    pe.matmul(out_ap, a_hi, b_hi, start=(first and n == 0), stop=False)
                    pe.matmul(out_ap, a_lo, b_hi, start=False, stop=False)
                    mm = pe.matmul(out_ap, a_hi, b_lo, start=False, stop=(last and n == len(terms) - 1))
                return mm

            def turn_x(b, t, bank):
                pe.wait_ge(s_ident, 2)
                when(pe, s_xn, TT * b + t + 1)
                for c in range(DC):
                    mm = pe.transpose(ps[:, bank, c * P:(c + 1) * P], xin[:, t, c * P:(c + 1) * P], ident[:])
                mm.then_inc(s_xt_mm, 1)

            def keys(j, chunks_of_k):
                c, h = j // 2, j % 2
                cols, toks = slice(c * P, (c + 1) * P), slice(h * JH, (h + 1) * JH)
                return three(ps[:, j % 8, 0:JH],
                             [(wkv_hi[:, 0, k, cols], wkv_lo[:, 0, k, cols], ctx_hi[:, k, toks], ctx_lo[:, k, toks])
                              for k in chunks_of_k], chunks_of_k[0] == 0, chunks_of_k[-1] == CC - 1)

            for k in range(CC):
                pe.wait_ge(s_ctx_lo, k + 1)
                pe.wait_ge(s_w_lo, k + 1)
                for j in range(8):
                    mm = keys(j, [k])
                    if k == CC - 1:
                        mm.then_inc(s_k_mm, 1)
            for j in range(8, 2 * NU):
                pe.wait_ge(s_k_lo, j - 7)
                keys(j, list(range(CC))).then_inc(s_k_mm, 1)
            pe.wait_ge(s_w_lo, 2 * CC)
            for i, (kind, n) in enumerate(ring):
                if i < 8:
                    pe.wait_ge(s_k_lo, 9 + i)
                else:
                    before, n_before = ring[i - 8]
                    if before == "x":
                        pe.wait_ge(s_xt_lo, n_before + 1)
                    else:
                        pe.wait_ge((s_v_act, s_v_dve)[n_before % 2], n_before // 2 + 1)
                if kind == "x":
                    turn_x(0, n, i % 8)
                    continue
                m, h = n // 2, n % 2
                rows = min(P, BJ - m * P)
                toks, cols = slice(m * P, m * P + rows), slice(h * 512, (h + 1) * 512)
                three(ps[0:rows, i % 8, :],
                      [(ctx_hi[:, k, toks], ctx_lo[:, k, toks], wkv_hi[:, 1, k, cols], wkv_lo[:, 1, k, cols])
                       for k in range(CC)], True, True).then_inc(s_v_mm, 1)
            pe.wait_ge(s_v_act, VT)
            pe.wait_ge(s_v_dve, VT)
            pe.wait_ge(s_w_lo, W_O)

            def scores(b, u, half):
                for tt in range(2):
                    toks = slice((2 * half + tt) * P, (2 * half + tt + 1) * P)
                    mm = three(ps[:, SCORE, tt * W2:(tt + 1) * W2],
                               [(q_hi[:, toks], q_lo[:, toks], k_bd[:, 0, u, :], k_bd[:, 1, u, :])], True, True)
                mm.then_inc(s_s_mm, 1)

            def turn_z(b, t, bank):
                when(pe, s_zn, TT * (b - 1) + t + 1)
                for c in range(DC):
                    mm = pe.transpose(ps[:, bank, c * P:(c + 1) * P], zn[:, t % 2, c * P:(c + 1) * P], ident[:])
                mm.then_inc(s_zt_mm, 1)

            def feed_forward(b, t, bank):
                when(pe, s_zt_lo, TT * (b - 1) + t + 1)
                i = t % 2
                three(ps[:, bank, :], [(zt_hi[:, i, c, :], zt_lo[:, i, c, :], wf_hi[:, c, :], wf_lo[:, c, :])
                                       for c in range(DC)], True, True).then_inc(s_f_mm, 1)

            def slot(b, u):
                cur, nxt, prev = has(b)
                g = b * NU + u
                pv, vu = unit_back(b, u, 2)
                yv, yu = unit_back(b, u, 3)
                if cur:
                    if nxt and u in (2, 4):
                        when(pe, s_xt_lo, TT * (b + 1) + {2: 1, 4: 4}[u])
                    if prev and u in (6, 7):
                        when(pe, s_zt_lo, TT * (b - 1) + u - 4)
                    if u == 0:
                        when(pe, s_xt_lo, TT * (b + 1))
                    par = b % 2
                    cols = slice(u * P, (u + 1) * P)
                    three(ps[:, WORK, :], [(wq_hi[:, c, cols], wq_lo[:, c, cols], xt_hi[:, par, c, :], xt_lo[:, par, c, :])
                                           for c in range(DC)], True, True).then_inc(s_q_mm, 1)
                if pv:
                    when(pe, s_masked, 2 * g if cur else 2 * NU * B)
                    if not cur:
                        when(pe, s_o_lo, g - 2)
                    when(pe, s_prob, g - 1)
                    for e in range(2):
                        for t in range(TT):
                            mm = pe.transpose(ps[0:JN, WORK + 1 + e, t * P:(t + 1) * P],
                                              prob[:, u % 2, 2 * t + e, :], ident[:])
                        mm.then_inc(s_pt_mm, 1)
                if yv:
                    when(pe, s_o_lo, g - 2)
                    if yu % 2 == 0 and not (isinstance(b, int) and b > 1):
                        pe.wait_ge(s_w_lo, W_O + yu // 2 + 1)
                    for t in range(TT):
                        if yu == 0 and not (isinstance(b, int) and b == 0):
                            when(pe, s_y, TT * (b - 1) + t + 1)
                        toks = slice(t * P, (t + 1) * P)
                        three(ps[:, t, :], [(o_hi[:, toks], o_lo[:, toks], wo_hi[:, yu, :], wo_lo[:, yu, :])],
                              yu == 0, yu == NU - 1).then_inc(s_y_mm, 1)
                if cur:
                    if u % HALF == 0:
                        when(pe, s_k_in[u // HALF], 64 * (b + 1))
                        if isinstance(b, int) and b == 0:
                            pe.wait_ge(s_null, 1)
                    if u < 2 and not pv:
                        when(pe, s_masked, 2 * g)
                    when(pe, s_q_lo, g + 1)
                    for t in X_TURN_5.get(u, []) if nxt else []:
                        turn_x(b + 1, t, WORK)
                    if prev and u >= 5:
                        turn_z(b, u - 4, WORK)
                    scores(b, u, 0)
                if pv:
                    when(pe, s_pt, 2 * (g - 1))
                    if vu % HALF == 0:
                        vb = b if u >= 2 else b - 1
                        when(pe, s_v_in[vu // HALF], 16 * (vb + 1))
                        if isinstance(b, int) and b == 0:
                            pe.wait_ge(s_null_v, 16)
                    for e in range(2):
                        cols = slice(vu * P + e * DH, vu * P + (e + 1) * DH)
                        mm = pe.matmul(ps[DH * e:DH * (e + 1), WORK + 1, :], v_sb[:, cols], p_t[:, e, :],
                                       start=True, stop=True)
                    mm.then_inc(s_pv_mm, 1)
                for t in X_TURN_7.get(u, []) if nxt else []:
                    turn_x(b + 1, t, WORK + 2)
                if prev and u == 4:
                    turn_z(b, 0, WORK + 2)
                if prev and u >= 5:
                    if u == 5 and not (isinstance(b, int) and b > 1):
                        pe.wait_ge(s_w_lo, W_END)
                    feed_forward(b, u - 5, WORK + 2)
                    if u == 7:
                        when(pe, s_o_lo, g - 1)
                        feed_forward(b, 3, WORK + 1)
                if cur:
                    when(pe, s_masked, 2 * g + 1)
                    scores(b, u, 1)

            run(pe, slot)
            turn_z(B, 0, SCORE)
            for t in range(TT):
                if t + 1 < TT:
                    turn_z(B, t + 1, SCORE + t + 1)
                pe.wait_ge(s_y, TT * (B - 1) + t + 1)
                feed_forward(B, t, t)

        @block.scalar
        def _(act):
            def split_hi(n):
                hi, _, factor = parts_of(n)
                act.wait_ge(s_stage_in[n % 3], 16 * (n // 3 + 1))
                if n == W_Q:
                    act.wait_ge(s_gn_in, 16)
                if factor is None:
                    act.activation(hi, stage_of(n), ACT.Copy).then_inc(s_w_hi, 1)
                else:
                    act.activation(hi, stage_of(n), ACT.Copy, scale=factor).then_inc(s_w_hi, 1)

            def x_hi(b, t, bank):
                when(act, s_xt_mm, TT * b + t + 1)
                act.activation(xt_hi[:, b % 2, :, t * P:(t + 1) * P],
                               ps[:, bank, :].rearrange("p (c n) -> p c n", c=DC), ACT.Copy).then_inc(s_xt_hi, 1)

            act.dma_start(route[:, 0, :], ffn_logits.rearrange("(a e) -> a e", a=1)).then_inc(s_route_in, 16)
            act.dma_start(route[:, 1, :], ffn_u.rearrange("(a e) -> a e", a=1)).then_inc(s_route_in, 16)
            for c in range(CC):
                act.wait_ge(s_ctx_in[c], 16)
                act.activation(ctx_hi[:, c, :], ctx_in[:, c, :], ACT.Copy).then_inc(s_ctx_hi, 1)
                split_hi(c)
            act.wait_ge(s_route_in, 32)
            act.activation(route[:, 2, :], route[:, 1, :], ACT.Ln).then_inc(s_ra, 1)
            act.wait_ge(s_ra, 1)
            act.activation(route[:, 3, :], route[:, 2, :], ACT.Ln, scale=-1.0).then_inc(s_ra, 1)
            act.wait_ge(s_rd, 1)
            act.activation(route[:, 4, :], route[:, 0, :], ACT.Exp, bias=route[:, 8, 0:1],
                           accum_out=route[:, 9, 0:1]).then_inc(s_ra, 1)
            act.wait_ge(s_ra, 3)
            act.activation(route[:, 9, 1:2], route[:, 9, 0:1], ACT.Ln).then_inc(s_ra, 1)
            act.wait_ge(s_const_in, 32)
            act.activation(tanh_g[:], gates[:], ACT.Tanh).then_inc(s_tanh, 1)
            for n in range(CC, CC + EARLY_V):
                split_hi(n)
            for j in range(2 * NU):
                c, h = j // 2, j % 2
                if c >= 2:
                    act.wait_ge(s_k_out[c % 2], 32 * (c // 2))
                act.wait_ge(s_k_mm, j + 1)
                act.activation(k_st[:, c % 2, 0, h * JH:(h + 1) * JH], ps[:, j % 8, 0:JH], ACT.Copy,
                               scale=DH ** -0.5).then_inc(s_k_hi, 1)
                if j in KEY_SPLITS:
                    split_hi(KEY_SPLITS[j])
            for i, (kind, n) in enumerate(ring):
                if kind == "x":
                    x_hi(0, n, i % 8)
                elif n % 2 == 0:
                    m = n // 2
                    rows = min(P, BJ - m * P)
                    if m >= 2:
                        act.wait_ge(s_v_out[m % 2], 16 * (m // 2))
                    act.wait_ge(s_v_mm, n + 1)
                    act.activation(v_st[0:rows, m % 2, 0:512], ps[0:rows, i % 8, :], ACT.Copy).then_inc(s_v_act, 1)
                if i in RING_SPLITS:
                    split_hi(RING_SPLITS[i])
            act.wait_ge(s_kz, 2)
            act.wait_ge(s_null_in, 32)
            for e in range(2):
                rows = slice(DH * e, DH * (e + 1))
                act.activation(k_bd[rows, 0, :, JN * e + J], null_k[rows, 0:1].to_broadcast([DH, NU]), ACT.Copy,
                               scale=DH ** -0.5).then_inc(s_null_hi, 1)

            def y_out(b, t):
                when(act, s_y_mm, TT * (b * NU - 1) + t + 1)
                act.activation(row[:, t, :], ps[:, t, :], ACT.Copy).then_inc(s_y, 1)

            def norm_z(b, t):
                when(act, s_z_nmr, TT * (b - 1) + t + 1)
                act.activation(zn[:, t % 2, :], row[:, t, :], ACT.Identity, bias=z_nmr[:, t:t + 1],
                               scale=z_rstd[:, t:t + 1]).then_inc(s_zn, 1)

            def z_hi(b, t, bank):
                when(act, s_zt_mm, TT * (b - 1) + t + 1)
                if t >= 2:
                    when(act, s_f_mm, TT * (b - 1) + t - 1)
                act.activation(zt_hi[:, t % 2, :, :], ps[:, bank, :].rearrange("p (c n) -> p c n", c=DC),
                               ACT.Copy).then_inc(s_zt_hi, 1)

            def slot(b, u):
                cur, nxt, prev = has(b)
                g = b * NU + u
                sv, _ = unit_back(b, u, 1)
                pv, _ = unit_back(b, u, 2)
                if prev and u >= 5:
                    norm_z(b, u - 4)
                if cur:
                    when(act, s_s_mm, 2 * g)
                    when(act, s_q_mm, g + 1)
                    act.activation(q_hi[:], ps[:, WORK, :], ACT.Copy).then_inc(s_q_hi, 1)
                if sv:
                    when(act, s_sub, g)
                    i = (u - 1) % 2
                    act.activation(prob[:, i, :, :], prob[:, i, :, :], ACT.Exp).then_inc(s_exp, 1)
                if pv:
                    when(act, s_pv_mm, g - 2)
                    for e in range(2):
                        when(act, s_pt_mm, 2 * (g - 2) + e + 1)
                        act.activation(p_t[:, e, :], ps[0:JN, WORK + 1 + e, :], ACT.Copy).then_inc(s_pt, 1)
                if prev and u == 4:
                    norm_z(b, 0)
                if prev and u == 2:
                    when(act, s_res_in, 16 * b)
                    for t in range(3):
                        y_out(b, t)
                for t in X_TURN_5.get(u, []) if nxt else []:
                    x_hi(b + 1, t, WORK)
                if prev and u >= 5:
                    z_hi(b, u - 4, WORK)
                if pv:
                    when(act, s_y_mm, TT * (g - 2))
                    when(act, s_pv_mm, g - 1)
                    act.activation(o_hi[:], ps[:, WORK + 1, :], ACT.Copy).then_inc(s_o_hi, 1)
                for t in X_TURN_7.get(u, []) if nxt else []:
                    x_hi(b + 1, t, WORK + 2)
                if prev and u == 4:
                    z_hi(b, 0, WORK + 2)
                if prev and u == 2:
                    y_out(b, 3)
                for n in splits_in(b, u):
                    if n == W_O:
                        act.wait_ge(s_v_mm, 2 * VT)
                    split_hi(n)

            run(act, slot)
            when(act, s_res_in, 16 * B)
            for t in range(TT):
                y_out(B, t)
            for t in range(TT):
                norm_z(B, t)
                z_hi(B, t, SCORE + t)

        @block.vector
        def _(dve):
            def split_lo(n):
                hi, lo, factor = parts_of(n)
                dve.wait_ge(s_w_hi, n + 1)
                if factor is None:
                    dve.tensor_tensor(lo, stage_of(n), hi.bitcast(F32), ALU.subtract).then_inc(s_w_lo, 1)
                else:
                    dve.scalar_tensor_tensor(out=lo, in0=stage_of(n), scalar=factor, in1=hi.bitcast(F32),
                                             op0=ALU.mult, op1=ALU.subtract).then_inc(s_w_lo, 1)

            def after(semaphore, count):
                if not isinstance(count, int):
                    count = dve.snap(dve.to_reg(count))
                    dve.wait_ge(s_ctx_lo, 1)
                dve.wait_ge(semaphore, count)

            def x_stats(b, t):
                dve.wait_ge(s_x_in[t], 16 * (b + 1))
                dve.bn_stats(x_stat[:, t, :], xin[:, t, :]).then_inc(s_x_bn, 1)
                after(s_x_bn, TT * b + t + 1)
                dve.bn_aggr(x_mv[:, t, :], x_stat[:, t, :]).then_inc(s_x_mv, 1)
                dve.wait_ge(s_x_mv, TT * b + t + 1)
                dve.tensor_scalar(x_var[:, t:t + 1], x_mv[:, t, 1:2], 1.0 + EPS, EPS * EPS,
                                  ALU.mult, ALU.add).then_inc(s_x_var, 1)

            def x_norm(b, t):
                when(dve, s_x_rstd, TT * b + t + 1)
                dve.tensor_scalar(xin[:, t, :], xin[:, t, :], x_mv[:, t, 0:1], x_rstd[:, t:t + 1],
                                  ALU.subtract, ALU.mult).then_inc(s_xn, 1)

            def x_lo(b, t, bank):
                when(dve, s_xt_hi, TT * b + t + 1)
                cols = slice(t * P, (t + 1) * P)
                dve.tensor_tensor(xt_lo[:, b % 2, :, cols], ps[:, bank, :].rearrange("p (c n) -> p c n", c=DC),
                                  xt_hi[:, b % 2, :, cols].bitcast(F32), ALU.subtract).then_inc(s_xt_lo, 1)

            dve.memset(k_bd[:, 0].bitcast(F32), 0.0).then_inc(s_kz, 1)
            dve.memset(k_bd[:, 1].bitcast(F32), 0.0).then_inc(s_kz, 1)
            for c in range(CC):
                dve.wait_ge(s_ctx_hi, c + 1)
                dve.tensor_tensor(ctx_lo[:, c, :], ctx_in[:, c, :], ctx_hi[:, c, :].bitcast(F32),
                                  ALU.subtract).then_inc(s_ctx_lo, 1)
                split_lo(c)
                if c == CC - 1:
                    dve.wait_ge(s_route_in, 32)
                    dve.tensor_reduce(route[:, 8, 0:1], route[:, 0, :], AX.X, ALU.max, negate=True).then_inc(s_rd, 1)
            dve.memset(mask_bias[:], 0.0).then_inc(s_rd, 1)
            dve.wait_ge(s_ra, 4)
            dve.wait_ge(s_rd, 2)
            dve.tensor_scalar(route[:, 5, :], route[:, 0, :], route[:, 8, 0:1], route[:, 9, 1:2],
                              ALU.add, ALU.subtract).then_inc(s_rd, 1)
            dve.wait_ge(s_mask_in, 16)
            dve.tensor_scalar(mask_bias[:, :, 0:J], mask_u8[:].rearrange("p (b j) -> p b j", b=B), 1.0, MASKED,
                              ALU.subtract, ALU.mult).then_inc(s_mask, 1)
            dve.wait_ge(s_rd, 3)
            dve.tensor_tensor(route[:, 6, :], route[:, 5, :], route[:, 3, :], ALU.subtract).then_inc(s_rd, 1)
            dve.wait_ge(s_rd, 4)
            dve.max(route[:, 7, :], route[:, 6, :]).then_inc(s_rd, 1)
            dve.wait_ge(s_rd, 5)
            dve.max_index(route_i[:], route[:, 7, :], route[:, 6, :]).then_inc(s_expert, 1)
            for n in range(CC, CC + EARLY_V):
                split_lo(n)
            for j in range(2 * NU):
                c, h = j // 2, j % 2
                dve.wait_ge(s_k_hi, j + 1)
                toks = slice(h * JH, (h + 1) * JH)
                dve.scalar_tensor_tensor(out=k_st[:, c % 2, 1, toks], in0=ps[:, j % 8, 0:JH], scalar=DH ** -0.5,
                                         in1=k_st[:, c % 2, 0, toks].bitcast(F32), op0=ALU.mult,
                                         op1=ALU.subtract).then_inc(s_k_lo, 1)
                if j in KEY_SPLITS:
                    split_lo(KEY_SPLITS[j])
                if j in (8, 10, 12, 14):
                    x_stats(0, j // 2 - 4)
            for i, (kind, n) in enumerate(ring):
                if i < TT:
                    x_norm(0, i)
                if kind == "x":
                    x_lo(0, n, i % 8)
                elif n % 2 == 1:
                    m = n // 2
                    rows = min(P, BJ - m * P)
                    if m >= 2:
                        dve.wait_ge(s_v_out[m % 2], 16 * (m // 2))
                    dve.wait_ge(s_v_mm, n + 1)
                    dve.tensor_copy(v_st[0:rows, m % 2, 512:1024], ps[0:rows, i % 8, :]).then_inc(s_v_dve, 1)
                if i in RING_SPLITS:
                    split_lo(RING_SPLITS[i])
            dve.wait_ge(s_null_hi, 2)
            for e in range(2):
                rows = slice(DH * e, DH * (e + 1))
                nl = dve.scalar_tensor_tensor(out=k_bd[rows, 1, :, JN * e + J], in0=null_k[rows, 0:1].to_broadcast([DH, NU]),
                                              scalar=DH ** -0.5, in1=k_bd[rows, 0, :, JN * e + J].bitcast(F32),
                                              op0=ALU.mult, op1=ALU.subtract)
            nl.then_inc(s_null, 1)
            dve.wait_ge(s_gout_in, 16)
            dve.wait_ge(s_tanh, 1)
            dve.tensor_scalar(gout[:], gout[:], tanh_g[:, 0:1], None, ALU.mult)

            def y_stats(b, tiles):
                for t in tiles:
                    when(dve, s_y, TT * (b - 1) + t + 1)
                    dve.bn_stats(y_stat[:, t, :], row[:, t, :]).then_inc(s_y_bn, 1)

            def y_moments(b, tiles):
                after(s_y_bn, TT * (b - 1) + tiles[-1] + 1)
                for t in tiles:
                    dve.bn_aggr(y_mv[:, t, :], y_stat[:, t, :]).then_inc(s_y_mv, 1)
                dve.wait_ge(s_y_mv, TT * (b - 1) + tiles[-1] + 1)
                span = slice(tiles[0], tiles[-1] + 1)
                dve.tensor_scalar(y_var[:, span], y_mv[:, span, 1], EPS, None, ALU.add).then_inc(s_y_var, 1)

            def y_gain(b, t):
                dve.scalar_tensor_tensor(out=row[:, t, :], in0=row[:, t, :], scalar=y_mv[:, t, 0:1], in1=gout[:],
                                         op0=ALU.subtract, op1=ALU.mult).then_inc(s_yg, 1)

            def x1(b, t, powers):
                when(dve, s_y_rstd, powers)
                dve.wait_ge(s_yg, TT * (b - 1) + t + 1)
                dve.scalar_tensor_tensor(out=row[:, t, :], in0=row[:, t, :], scalar=y_rstd[:, t:t + 1],
                                         in1=x_res[:, t, :], op0=ALU.mult, op1=ALU.add).then_inc(s_x1, 1)

            def x1_stats(b, t):
                dve.wait_ge(s_x1, TT * (b - 1) + t + 1)
                dve.bn_stats(z_stat[:, t, :], row[:, t, :]).then_inc(s_z_bn, 1)
                after(s_z_bn, TT * (b - 1) + t + 1)
                dve.bn_aggr(z_mv[:, t, :], z_stat[:, t, :]).then_inc(s_z_mv, 1)
                dve.wait_ge(s_z_mv, TT * (b - 1) + t + 1)
                dve.tensor_scalar(z_var[:, t:t + 1], z_mv[:, t, 1:2], EPS, None, ALU.add).then_inc(s_z_var, 1)

            def z_shift(b, t):
                when(dve, s_z_rstd, TT * (b - 1) + t + 1)
                dve.scalar_tensor_tensor(out=z_nmr[:, t:t + 1], in0=z_mv[:, t, 0:1], scalar=-1.0,
                                         in1=z_rstd[:, t:t + 1], op0=ALU.mult, op1=ALU.mult).then_inc(s_z_nmr, 1)

            def z_lo(b, t, bank):
                when(dve, s_zt_hi, TT * (b - 1) + t + 1)
                dve.tensor_tensor(zt_lo[:, t % 2, :, :], ps[:, bank, :].rearrange("p (c n) -> p c n", c=DC),
                                  zt_hi[:, t % 2, :, :].bitcast(F32), ALU.subtract).then_inc(s_zt_lo, 1)

            def result(b, t, bank):
                when(dve, s_x1b, TT * (b - 1) + t + 1)
                when(dve, s_f_mm, TT * (b - 1) + t + 1)
                dve.tensor_tensor(row[:, t, :], ps[:, bank, :], row[:, t, :], ALU.add).then_inc(s_res, 1)

            def unmask(b, u, half):
                when(dve, s_s_mm, 2 * (b * NU + u) + half + 1)
                dve.tensor_tensor(prob[:, u % 2, 4 * half:4 * half + 4, :], psum_scores,
                                  mask_bias[:, bass.ds(b, 1), :].to_broadcast([P, 4, JN]),
                                  ALU.add).then_inc(s_masked, 1)

            def slot(b, u):
                cur, nxt, prev = has(b)
                g = b * NU + u
                sv, _ = unit_back(b, u, 1)
                pv, _ = unit_back(b, u, 2)
                if prev and u == 3:
                    y_stats(b, [2, 3])
                    y_moments(b, [0, 1, 2, 3])
                if prev and u == 4:
                    x1_stats(b, 0)
                if prev and u >= 5:
                    z_shift(b, u - 4)
                if prev and u in (4, 5, 6):
                    y_gain(b, u - 3)
                    x1(b, u - 3, b)
                for t in X_NORM_A.get(u, []) if nxt else []:
                    x_norm(b + 1, t)
                for t in X_STATS_A.get(u, []) if nxt else []:
                    x_stats(b + 1, t)
                if cur:
                    when(dve, s_q_hi, g + 1)
                    dve.tensor_tensor(q_lo[:], ps[:, WORK, :], q_hi[:].bitcast(F32), ALU.subtract)\
                        .then_inc(s_q_lo, 1)
                if sv:
                    when(dve, s_exp, g)
                    dve.tensor_reduce(s_sum[:], prob[:, (u - 1) % 2, :, :], AX.X, ALU.add).then_inc(s_sum_ok, 1)
                    when(dve, s_sum_ok, g)
                    when(dve, s_prob, g - 1)
                    dve.reciprocal(s_rcp[:], s_sum[:]).then_inc(s_rcp_ok, 1)
                if prev and u == 4:
                    z_shift(b, 0)
                if prev and u in (4, 5, 6):
                    x1_stats(b, u - 3)
                if prev and u == 3:
                    y_gain(b, 0)
                    x1(b, 0, b)
                for t in X_STATS_B.get(u, []) if nxt else []:
                    x_stats(b + 1, t)
                for t in X_NORM_B.get(u, []) if nxt else []:
                    x_norm(b + 1, t)
                if isinstance(b, int) and b == 0 and u == 5:
                    dve.wait_ge(s_bias_in, 16)
                    dve.tensor_scalar(bias[:], bias[:], tanh_g[:, 1:2], None, ALU.mult).then_inc(s_bias, 1)
                if cur:
                    if u == 0 and isinstance(b, int) and b == 0:
                        dve.wait_ge(s_mask, 1)
                    when(dve, s_pt_mm, 2 * (g - 1))
                    unmask(b, u, 0)
                for t in X_TURN_5.get(u, []) if nxt else []:
                    x_lo(b + 1, t, WORK)
                if prev and u >= 5:
                    z_lo(b, u - 4, WORK)
                if prev and u == 2:
                    y_stats(b, [0, 1])
                if pv:
                    when(dve, s_o_hi, g - 1)
                    dve.tensor_tensor(o_lo[:], ps[:, WORK + 1, :], o_hi[:].bitcast(F32), ALU.subtract)\
                        .then_inc(s_o_lo, 1)
                for t in X_TURN_7.get(u, []) if nxt else []:
                    x_lo(b + 1, t, WORK + 2)
                if prev and u == 4:
                    z_lo(b, 0, WORK + 2)
                if prev and u >= 5:
                    result(b, u - 5, WORK + 2)
                if prev and u == 7:
                    result(b, 3, WORK + 1)
                if cur:
                    unmask(b, u, 1)
                    when(dve, s_masked, 2 * g + 2)
                    dve.tensor_reduce(s_top[:], prob[:, u % 2, :, :], AX.X, ALU.max).then_inc(s_top_ok, 1)
                for n in splits_in(b, u):
                    split_lo(n)

            run(dve, slot)
            def lag(t):
                y_stats(B, [t])
                y_moments(B, [t])

            lag(0)
            y_gain(B, 0)
            lag(1)
            for t in range(TT):
                x1(B, t, B + t)
                if t:
                    z_shift(B, t - 1)
                x1_stats(B, t)
                if t + 2 < TT:
                    lag(t + 2)
                if t:
                    z_lo(B, t - 1, SCORE + t - 1)
                if t + 1 < TT:
                    y_gain(B, t + 1)
                if t == TT - 1:
                    z_shift(B, t)
                if t > 1:
                    result(B, t - 2, t - 2)
            z_lo(B, TT - 1, SCORE + TT - 1)
            result(B, TT - 2, TT - 2)
            result(B, TT - 1, TT - 1)

        @block.gpsimd
        def _(pool):
            def spread(ap):
                return ap.rearrange("p (g o) -> p g o", o=1).to_broadcast([P, 2 * TT, JN])

            def x_power(b, t):
                when(pool, s_x_var, TT * b + t + 1)
                pool.tensor_tensor(x_rstd[:, t:t + 1], x_var[:, t:t + 1], half_neg[:, 0:1], ALU.pow)\
                    .then_inc(s_x_rstd, 1)
            def z_power(b, t):
                when(pool, s_z_var, TT * (b - 1) + t + 1)
                pool.tensor_tensor(z_rstd[:, t:t + 1], z_var[:, t:t + 1], half_neg[:, 0:1], ALU.pow)\
                    .then_inc(s_z_rstd, 1)

            def add_bias(b, t):
                when(pool, s_zn, TT * (b - 1) + t + 1)
                pool.tensor_tensor(row[:, t, :], row[:, t, :], bias[:], ALU.add).then_inc(s_x1b, 1)

            pool.dma_start(gates[:, 0:1], g_xattn.partition_broadcast(P)).then_inc(s_const_in, 16)
            pool.dma_start(gates[:, 1:2], g_ffn.partition_broadcast(P)).then_inc(s_const_in, 16)
            for e in range(2):
                pool.dma_start(null_k[DH * e:DH * (e + 1), :], null_kv[0].rearrange("(d o) -> d o", o=1))\
                    .then_inc(s_null_in, 16)
            pool.dma_start(v_sb[J:JN, :].rearrange("a (h d) -> a h d", d=DH),
                          null_kv[1:2, :].rearrange("a (h d) -> a h d", h=1).to_broadcast([1, INNER // DH, DH]))\
                .then_inc(s_null_v, 16)
            pool.dma_start(mask_u8[:], mask.rearrange("b j -> (b j)").partition_broadcast(P)).then_inc(s_mask_in, 16)
            pool.dma_start(gout[:], g_out.partition_broadcast(P)).then_inc(s_gout_in, 16)
            pool.memset(half_neg[:], -0.5)
            pool.memset(ident[:], 0.0).then_inc(s_ident, 1)
            pool.wait_ge(s_ident, 1)
            pool.affine_select(out=ident[:], in_=ident[:], compare_op=ALU.not_equal, fill=1.0, base=0,
                               pattern=[[-1, P]], channel_multiplier=1).then_inc(s_ident, 1)
            for t in range(TT):
                x_power(0, t)

            def slot(b, u):
                cur, nxt, prev = has(b)
                g = b * NU + u
                sv, _ = unit_back(b, u, 1)
                i = (u - 1) % 2
                if sv:
                    when(pool, s_top_ok, g)
                    pool.tensor_tensor(prob[:, i, :, :], prob[:, i, :, :], spread(s_top[:]), ALU.subtract)\
                        .then_inc(s_sub, 1)
                if prev and u == 3:
                    when(pool, s_y_var, b)
                    pool.tensor_tensor(y_rstd[:], y_var[:], half_neg[:], ALU.pow).then_inc(s_y_rstd, 1)
                if prev and u == 4:
                    z_power(b, 0)
                if sv:
                    when(pool, s_rcp_ok, g)
                    pool.tensor_tensor(prob[:, i, :, :], prob[:, i, :, :], spread(s_rcp[:]), ALU.mult)\
                        .then_inc(s_prob, 1)
                for t in {0: [0, 1], 1: [2, 3]}.get(u, []) if nxt else []:
                    x_power(b + 1, t)
                if prev and u >= 4:
                    if u == 4 and not (isinstance(b, int) and b > 1):
                        pool.wait_ge(s_bias, 1)
                    add_bias(b, u - 4)
                if prev and 4 <= u < 7:
                    z_power(b, u - 3)

            run(pool, slot)
            def y_power(t):
                pool.wait_ge(s_y_var, B + t)
                pool.tensor_tensor(y_rstd[:, t:t + 1], y_var[:, t:t + 1], half_neg[:, 0:1], ALU.pow)\
                    .then_inc(s_y_rstd, 1)
            y_power(0)
            y_power(1)
            for t in range(TT):
                if t + 2 < TT:
                    y_power(t + 2)
                z_power(B, t)
                if t:
                    add_bias(B, t - 1)
            add_bias(B, TT - 1)


_INS = ["x", "ctx_768", "mask_BxS2_bf1", "g_xattn", "g_ffn", "L0_xattn_g_norm", "L0_xattn_null_kv", "L0_xattn_Wq",
        "L0_xattn_Wkv", "L0_xattn_Wout", "L0_xattn_g_out", "L0_ffn_W", "L0_ffn_b", "L0_ffn_logits", "L0_ffn_u"]


def kernel(**inputs):
    import numpy as np
    import concourse.bacc as bacc
    from concourse import mybir as mb
    from concourse.bass_utils import run_bass_kernel_spmd

    nc = bacc.Bacc("TRN2", target_bir_lowering=False, num_devices=1)
    arrays, args = {}, []
    for name in _INS:
        a = np.asarray(inputs[name])
        if name == "ctx_768":
            a = a.reshape(-1, a.shape[-1]).T
        if name == "L0_xattn_g_norm":
            a = a.reshape(-1, P).T
        a = np.ascontiguousarray(a)
        if a.dtype == np.bool_:
            a = a.view(np.uint8)
        arrays[f"in_{name}"] = a
        args.append(nc.dram_tensor(f"in_{name}", a.shape, mb.dt.from_np(a.dtype), kind="ExternalInput").ap())
    shape = inputs["x"].shape
    args.append(nc.dram_tensor("out_0", shape, mb.dt.float32, kind="ExternalOutput").ap())
    flamingo_program(nc, *args)
    r = run_bass_kernel_spmd(nc, [arrays], core_ids=[0])
    return r.results[0]["out_0"]
```

```python
from contextlib import ExitStack

import concourse.bass as bass
from concourse import mybir

F32 = mybir.dt.float32
F32R = mybir.dt.float32r
U32 = mybir.dt.uint32
U8 = mybir.dt.uint8
ALU = mybir.AluOpType
ACT = mybir.ActivationFunctionType
AX = mybir.AxisListType

P = 128
EPS = 1e-5
MASKED = 3.0e38
DH = 64


def flamingo_program(nc, x, ctx_t, mask, g_xattn, g_ffn, g_norm, null_kv, w_q, w_kv, w_out, g_out,
                     ffn_w, ffn_b, ffn_logits, ffn_u, out):
    B, N, D = x.shape
    C, BJ = ctx_t.shape
    J = BJ // B
    JN = J + 1
    INNER = w_q.shape[1]
    E = ffn_w.shape[0]
    TT = N // P
    DC = D // P
    CC = C // P
    NU = INNER // P
    HALF = NU // 2
    W2 = 2 * JN
    JH = BJ // 2
    KB = 6
    VT = (BJ + P - 1) // P
    assert (TT, DC, NU) == (4, 4, 8) and N == 512 and D == 512 and BJ % 2 == 0

    x_tok = x.rearrange("b n d -> (b n) d")
    out_tok = out.rearrange("b n d -> (b n) d")

    stack = ExitStack()

    def sb(name, shape, dt=F32):
        return stack.enter_context(nc.sbuf_tensor(name, shape, dt))

    def sem(name):
        return stack.enter_context(nc.semaphore(name))

    k_dram = nc.dram_tensor("k_dram", (INNER, BJ), F32, kind="Internal").ap()
    v_dram = nc.dram_tensor("v_dram", (BJ, INNER), F32, kind="Internal").ap()

    with stack:
        ps = stack.enter_context(nc.psum_tensor("ps", [P, 8, 512], F32))
        SCORE, WORK = 4, 5

        wq_hi = sb("wq_hi", [P, DC, INNER], F32R)
        wq_lo = sb("wq_lo", [P, DC, INNER], F32R)
        xt_hi = sb("xt_hi", [P, 2, DC, N], F32R)
        xt_lo = sb("xt_lo", [P, 2, DC, N], F32R)
        k_bd = sb("k_bd", [P, 2, NU, W2], F32R)
        k_raw = sb("k_raw", [P, 2, HALF, J])
        v_sb = sb("v_sb", [JN, INNER])
        xin = sb("xin", [P, TT, D])
        stage = sb("stage", [P, 3, 1024])
        gout = sb("gout", [P, D])
        bias = sb("bias", [P, D])
        mask_bias = sb("mask_bias", [P, B, JN])
        ident = sb("ident", [P, P])
        gn = sb("gn", [P, DC])
        half_neg = sb("half_neg", [P, TT])
        gates = sb("gates", [P, 2])
        tanh_g = sb("tanh_g", [P, 2])
        null_k = sb("null_k", [P, 1])
        route = sb("route", [1, 10, 8])
        route_i = sb("route_i", [1, 8], U32)
        x_stat = sb("x_stat", [P, TT, 6])
        x_mv = sb("x_mv", [P, TT, 2])
        x_var = sb("x_var", [P, TT])
        x_rstd = sb("x_rstd", [P, TT])
        y_stat = sb("y_stat", [P, TT, 6])
        y_mv = sb("y_mv", [P, TT, 2])
        y_var = sb("y_var", [P, TT])
        y_rstd = sb("y_rstd", [P, TT])
        z_stat = sb("z_stat", [P, TT, 6])
        z_mv = sb("z_mv", [P, TT, 2])
        z_var = sb("z_var", [P, TT])
        z_rstd = sb("z_rstd", [P, TT])
        z_nmr = sb("z_nmr", [P, TT])
        s_top = sb("s_top", [P, 2 * TT])
        s_sum = sb("s_sum", [P, 2 * TT])
        s_rcp = sb("s_rcp", [P, 2 * TT])

        early = ExitStack()
        with early:
            def esb(name, shape, dt=F32):
                return early.enter_context(nc.sbuf_tensor(name, shape, dt))
            wk_hi = esb("wk_hi", [P, CC, INNER], F32R)
            wk_lo = esb("wk_lo", [P, CC, INNER], F32R)
            wv_hi = esb("wv_hi", [P, CC, INNER], F32R)
            wv_lo = esb("wv_lo", [P, CC, INNER], F32R)
            ctx_in = esb("ctx_in", [P, CC, BJ])
            k_st = esb("k_st", [P, KB, BJ])
            v_st = esb("v_st", [P, 2, INNER])
            ctx_hi = esb("ctx_hi", [P, CC, BJ], F32R)
            ctx_lo = esb("ctx_lo", [P, CC, BJ], F32R)
        wo_hi = sb("wo_hi", [P, NU, D], F32R)
        wo_lo = sb("wo_lo", [P, NU, D], F32R)
        wf_hi = sb("wf_hi", [P, DC, D], F32R)
        wf_lo = sb("wf_lo", [P, DC, D], F32R)
        q_hi = sb("q_hi", [P, N], F32R)
        q_lo = sb("q_lo", [P, N], F32R)
        prob = sb("prob", [P, 2, 2 * TT, JN])
        p_t = sb("p_t", [JN, 2, N])
        o_hi = sb("o_hi", [P, N], F32R)
        o_lo = sb("o_lo", [P, N], F32R)
        zn = sb("zn", [P, 2, D])
        row = sb("row", [P, TT, D])
        zt_hi = sb("zt_hi", [P, 2, DC, P], F32R)
        zt_lo = sb("zt_lo", [P, 2, DC, P], F32R)
        x_res = sb("x_res", [P, TT, D])
        mask_u8 = sb("mask_u8", [P, B * J], U8)

        s_ctx_in = [sem(f"s_ctx_in{c}") for c in range(CC)]
        s_gn_in = sem("s_gn_in")
        s_const_in = sem("s_const_in")
        s_route_in = sem("s_route_in")
        s_stage_in = [sem(f"s_stage_in{i}") for i in range(3)]
        s_x_in = [sem(f"s_x_in{t}") for t in range(TT)]
        s_res_in = sem("s_res_in")
        s_bias_in = sem("s_bias_in")
        s_k_in = [sem(f"s_k_in{h}") for h in range(2)]
        s_v_in = [sem(f"s_v_in{h}") for h in range(2)]
        s_k_out = [sem(f"s_k_out{i}") for i in range(KB)]
        s_v_out = [sem(f"s_v_out{i}") for i in range(2)]
        s_null_in = sem("s_null_in")
        s_null_v = sem("s_null_v")
        s_mask_in = sem("s_mask_in")
        s_gout_in = sem("s_gout_in")
        s_out = sem("s_out")
        s_ident = sem("s_ident")
        s_tanh = sem("s_tanh")
        s_ra = sem("s_ra")
        s_rd = sem("s_rd")
        s_expert = sem("s_expert")
        s_ctx_hi = sem("s_ctx_hi")
        s_ctx_lo = sem("s_ctx_lo")
        s_wk_hi = sem("s_wk_hi")
        s_wk_lo = sem("s_wk_lo")
        s_w_hi = sem("s_w_hi")
        s_w_lo = sem("s_w_lo")
        s_k_mm = sem("s_k_mm")
        s_k_act = sem("s_k_act")
        s_k_dve = sem("s_k_dve")
        s_v_mm = sem("s_v_mm")
        s_v_act = sem("s_v_act")
        s_v_dve = sem("s_v_dve")
        s_kz = sem("s_kz")
        s_null_hi = sem("s_null_hi")
        s_null = sem("s_null")
        s_mask = sem("s_mask")
        s_bias = sem("s_bias")
        s_q_mm = sem("s_q_mm")
        s_s_mm = sem("s_s_mm")
        s_pt_mm = sem("s_pt_mm")
        s_pv_mm = sem("s_pv_mm")
        s_y_mm = sem("s_y_mm")
        s_xt_mm = sem("s_xt_mm")
        s_zt_mm = sem("s_zt_mm")
        s_f_mm = sem("s_f_mm")
        s_k_hi = [sem(f"s_k_hi{h}") for h in range(2)]
        s_q_hi = sem("s_q_hi")
        s_exp = sem("s_exp")
        s_pt = sem("s_pt")
        s_o_hi = sem("s_o_hi")
        s_xt_hi = sem("s_xt_hi")
        s_y = sem("s_y")
        s_zn = sem("s_zn")
        s_zt_hi = sem("s_zt_hi")
        s_k_lo = [sem(f"s_k_lo{h}") for h in range(2)]
        s_q_lo = sem("s_q_lo")
        s_masked = sem("s_masked")
        s_top_ok = sem("s_top_ok")
        s_sum_ok = sem("s_sum_ok")
        s_rcp_ok = sem("s_rcp_ok")
        s_o_lo = sem("s_o_lo")
        s_xt_lo = sem("s_xt_lo")
        s_x_bn = sem("s_x_bn")
        s_x_mv = sem("s_x_mv")
        s_x_var = sem("s_x_var")
        s_y_bn = sem("s_y_bn")
        s_y_mv = sem("s_y_mv")
        s_y_var = sem("s_y_var")
        s_yg = sem("s_yg")
        s_x1 = sem("s_x1")
        s_z_bn = sem("s_z_bn")
        s_z_mv = sem("s_z_mv")
        s_z_var = sem("s_z_var")
        s_z_nmr = sem("s_z_nmr")
        s_zt_lo = sem("s_zt_lo")
        s_res = sem("s_res")
        s_sub = sem("s_sub")
        s_prob = sem("s_prob")
        s_x_rstd = sem("s_x_rstd")
        s_xn = sem("s_xn")
        s_y_rstd = sem("s_y_rstd")
        s_z_rstd = sem("s_z_rstd")
        s_x1b = sem("s_x1b")

        chunks = [w_kv[c * P:(c + 1) * P, h * INNER:(h + 1) * INNER] for h in range(2) for c in range(CC)]
        chunks += [w_q[c * P:(c + 1) * P, :] for c in range(DC)]
        chunks += [w_out[2 * c * P:2 * (c + 1) * P, :].rearrange("(a p) d -> p a d", p=P) for c in range(NU // 2)]
        W_K, W_V, W_Q, W_O = 0, CC, 2 * CC, 2 * CC + DC
        W_F = W_O + NU // 2
        W_END = W_F + DC // 2

        def stage_of(n):
            s = stage[:, n % 3, :]
            return s if n < W_O else s.rearrange("p (a d) -> p a d", a=2)

        def parts_of(n):
            if n < W_V:
                return wk_hi[:, n, :], wk_lo[:, n, :], None
            if n < W_Q:
                return wv_hi[:, n - W_V, :], wv_lo[:, n - W_V, :], None
            if n < W_O:
                c = n - W_Q
                return wq_hi[:, c, :], wq_lo[:, c, :], gn[:, c:c + 1]
            if n < W_F:
                c = 2 * (n - W_O)
                return wo_hi[:, c:c + 2, :], wo_lo[:, c:c + 2, :], None
            c = 2 * (n - W_F)
            return wf_hi[:, c:c + 2, :], wf_lo[:, c:c + 2, :], tanh_g[:, 1:2]

        LEFT, RIGHT = slice(0, INNER // 2), slice(INNER // 2, INNER)
        EARLY_V = 1
        KEY_SPLITS = {3: CC + 1, 7: CC + 2, 9: W_Q, 11: W_Q + 1, 12: W_Q + 2, 15: W_Q + 3}

        LATE_FF = (2, 3)

        def ends(b):
            return isinstance(b, int) and b == B - 1

        def last_unit(b, u, lag):
            return isinstance(b, int) and NU * b + u - lag == NU * B - 1

        def turned_bank(b, u):
            return SCORE if last_unit(b, u, 2) else WORK + 1

        def output_of(b, u, lag):
            return (q_hi, q_lo) if last_unit(b, u, lag) else (o_hi, o_lo)

        def spread(ap):
            return ap.rearrange("p (g o) -> p g o", o=1).to_broadcast([P, 2 * TT, JN])

        def value_rows(n):
            return n // 2, min(P, BJ - n // 2 * P)

        def when(engine, semaphore, count):
            if not isinstance(count, int) or count > 0:
                engine.wait_ge(semaphore, count)

        def splits_in(b, u):
            if isinstance(b, int) and b == 0:
                return {1: [W_O], 2: [W_O + 1], 4: [W_O + 2], 5: [W_O + 3], 6: [W_F], 7: [W_F + 1]}.get(u, [])
            return []

        def run(engine, slot):
            for u in range(NU):
                slot(0, u)
            with engine.Fori(1, B - 1) as b:
                for u in range(NU):
                    slot(b, u)
            for u in range(NU):
                slot(B - 1, u)
            for u in range(3):
                slot(B, u)

        def has(b):
            if isinstance(b, int):
                return b < B, b + 1 < B, 0 < b < B
            return True, True, True

        def unit_back(b, u, lag):
            there = not isinstance(b, int) or 0 <= NU * b + u - lag < NU * B
            return there, (u - lag) % NU

        X_STATS_A, X_STATS_B = {0: [0], 1: [2]}, {0: [1], 1: [3]}
        X_NORM_A, X_NORM_B = {1: [0], 2: [2, 3]}, {1: [1]}
        X_TURN_5, X_TURN_7 = {1: [0], 3: [3]}, {1: [1], 2: [2]}

        ring = [("v", 0), ("x", 0), ("x", 1), ("v", 1), ("x", 2), ("x", 3), ("v", 2), ("v", 3)]
        V_LATE = {0: (4, 5), 1: (6, 7), 2: (8, 9)}
        assert 2 * VT == 10 and TT == 4

        def x_slot(b, u):
            return u - 3 if isinstance(b, int) and b == 0 else u

        psum_scores = ps[:, SCORE, 0:2 * W2].rearrange("p (g j) -> p g j", j=JN)

        block = stack.enter_context(nc.Block())

        @block.sync
        def _(sp):
            def load_stage(n, src):
                if n >= 3:
                    sp.wait_ge(s_w_lo, n - 2)
                sp.dma_start(stage_of(n), src).then_inc(s_stage_in[n % 3], 16)

            def load_keys(b, h):
                src = k_dram[h * HALF * P:(h + 1) * HALF * P, bass.ds(b * J, J)]
                sp.dma_start(k_raw[:, h], src.rearrange("(u p) j -> p u j", p=P)).then_inc(s_k_in[h], 16)

            def load_values(b, h):
                cols = slice(h * HALF * P, (h + 1) * HALF * P)
                sp.dma_start(v_sb[0:J, cols], v_dram[bass.ds(b * J, J), cols]).then_inc(s_v_in[h], 16)

            def load_x(b, t):
                sp.dma_start(xin[:, t, :], x_tok[bass.ds(b * N + t * P, P), :]).then_inc(s_x_in[t], 16)

            for c in range(CC):
                sp.dma_start(ctx_in[:, c, :], ctx_t[c * P:(c + 1) * P, :]).then_inc(s_ctx_in[c], 16)
                load_stage(c, chunks[c])
            sp.dma_start(gn[:], g_norm).then_inc(s_gn_in, 16)
            for n in range(CC, W_Q):
                load_stage(n, chunks[n])
            for t in range(TT):
                load_x(0, t)
            for c in range(NU):
                sp.wait_ge(s_k_act, c + 1)
                sp.wait_ge(s_k_dve, c + 1)
                sp.dma_start(k_dram[c * P:(c + 1) * P, :], k_st[:, c % KB, :]).then_inc(s_k_out[c % KB], 16)
                if c == KB - 1:
                    for i in range(HALF):
                        sp.wait_ge(s_k_out[i], 16)
                    load_keys(0, 0)
                if c < DC:
                    load_stage(W_Q + c, chunks[W_Q + c])

            def store_values(m):
                rows = min(P, BJ - m * P)
                sp.wait_ge(s_v_act, m + 1)
                sp.wait_ge(s_v_dve, m + 1)
                sp.dma_start(v_dram[m * P:m * P + rows, :], v_st[0:rows, m % 2, :]).then_inc(s_v_out[m % 2], 16)

            for t in range(TT):
                sp.wait_ge(s_xt_mm, t + 1)
                load_x(1, t)
            store_values(0)
            store_values(1)
            for i in range(KB):
                sp.wait_ge(s_k_out[i], 32 if i + KB < NU else 16)
            load_keys(0, 1)
            sp.wait_ge(s_v_out[0], 16)
            for h in range(2):
                load_values(0, h)
            store_values(2)
            load_stage(W_O, chunks[W_O])
            store_values(3)
            load_stage(W_O + 1, chunks[W_O + 1])
            store_values(4)
            sp.wait_ge(s_expert, 1)
            expert = sp.value_load(route_i[0:1, 0:1], min_val=0, max_val=E - 1)
            sp.dma_start(bias[:], ffn_b[bass.ds(expert, 1), :].partition_broadcast(P)
                         .rearrange("p a d -> p (a d)")).then_inc(s_bias_in, 16)
            load_stage(W_O + 2, chunks[W_O + 2])
            load_stage(W_O + 3, chunks[W_O + 3])
            for c in range(DC // 2):
                src = ffn_w[bass.ds(expert, 1), 2 * c * P:2 * (c + 1) * P, :]
                load_stage(W_F + c, src.rearrange("a (c p) d -> p (a c) d", p=P))

            sp.wait_ge(s_v_out[0], 16 * ((VT + 1) // 2))
            sp.wait_ge(s_v_out[1], 16 * (VT // 2))

            def batch(b):
                cur, nxt, _ = has(b)
                prev = not (isinstance(b, int) and b == 0)
                if cur and prev:
                    when(sp, s_pv_mm, NU * b)
                    load_values(b, 1)
                if nxt:
                    for h in range(2):
                        when(sp, s_k_lo[h], 2 * (b + 1))
                        load_keys(b + 1, h)
                    if not (isinstance(b, int) and b + 2 >= B):
                        for t in range(TT):
                            when(sp, s_xt_mm, TT * (b + 1) + t + 1)
                            load_x(b + 2, t)
                    when(sp, s_pv_mm, NU * b + HALF)
                    load_values(b + 1, 0)
                if isinstance(b, int) and b == B:
                    for t in LATE_FF:
                        sp.wait_ge(s_res, TT * (B - 2) + t + 1)
                        sp.dma_start(out_tok[(B - 2) * N + t * P:(B - 2) * N + (t + 1) * P, :], xin[:, t, :])\
                            .then_inc(s_out, 16)
                if prev:
                    tiles = LATE_FF[0] if ends(b) else TT
                    for t in range(tiles):
                        when(sp, s_res, TT * (b - 1) + t + 1)
                        sp.dma_start(out_tok[bass.ds((b - 1) * N + t * P, P), :], row[:, t, :])\
                            .then_inc(s_out, 16)
                if cur:
                    if prev:
                        when(sp, s_out, 16 * (TT * (b - 1) + tiles))
                    sp.dma_start(x_res[:], x_tok[bass.ds(b * N, N), :].rearrange("(t p) d -> p t d", p=P))\
                        .then_inc(s_res_in, 16)

            batch(0)
            with sp.Fori(1, B - 2) as b:
                batch(b)
            batch(B - 2)
            batch(B - 1)
            batch(B)
            sp.wait_ge(s_out, 16 * TT * B)

        @block.tensor
        def _(pe):
            def three(out_ap, terms, first, last):
                mm = None
                for n, (a_hi, a_lo, b_hi, b_lo) in enumerate(terms):
                    pe.matmul(out_ap, a_hi, b_hi, start=(first and n == 0), stop=False)
                    pe.matmul(out_ap, a_lo, b_hi, start=False, stop=False)
                    mm = pe.matmul(out_ap, a_hi, b_lo, start=False, stop=(last and n == len(terms) - 1))
                return mm

            def turn_x(b, t, bank):
                pe.wait_ge(s_ident, 2)
                when(pe, s_xn, TT * b + t + 1)
                for c in range(DC):
                    mm = pe.transpose(ps[:, bank, c * P:(c + 1) * P], xin[:, t, c * P:(c + 1) * P], ident[:])
                mm.then_inc(s_xt_mm, 1)

            def keys(j, chunks_of_k):
                c, h = j // 2, j % 2
                cols, toks = slice(c * P, (c + 1) * P), slice(h * JH, (h + 1) * JH)
                return three(ps[:, (j + 2) % 8, 0:JH],
                             [(wk_hi[:, k, cols], wk_lo[:, k, cols], ctx_hi[:, k, toks], ctx_lo[:, k, toks])
                              for k in chunks_of_k], chunks_of_k[0] == 0, chunks_of_k[-1] == CC - 1)

            def values(n, bank):
                m, rows = value_rows(n)
                toks, cols = slice(m * P, m * P + rows), slice(n % 2 * 512, (n % 2 + 1) * 512)
                three(ps[0:rows, bank, :],
                      [(ctx_hi[:, k, toks], ctx_lo[:, k, toks], wv_hi[:, k, cols], wv_lo[:, k, cols])
                       for k in range(CC)], True, True).then_inc(s_v_mm, 1)

            for k in range(CC):
                pe.wait_ge(s_ctx_lo, k + 1)
                pe.wait_ge(s_wk_lo, k + 1)
                for j in range(8):
                    mm = keys(j, [k])
                    if k == CC - 1:
                        mm.then_inc(s_k_mm, 1)
            pe.wait_ge(s_w_lo, CC)
            for j in range(8, 2 * NU):
                pe.wait_ge((s_k_act, s_k_dve)[j % 2], (j - 8) // 2 + 1)
                keys(j, list(range(CC))).then_inc(s_k_mm, 1)
            pe.wait_ge(s_w_lo, 2 * CC)
            for i, (kind, n) in enumerate(ring):
                pe.wait_ge((s_k_act, s_k_dve)[i % 2], (8 + i) // 2 + 1)
                if kind == "x":
                    turn_x(0, n, (i + 2) % 8)
                    continue
                values(n, (i + 2) % 8)
            pe.wait_ge(s_v_dve, 1)
            pe.wait_ge(s_w_lo, W_O)

            def scores(b, u, half):
                for tt in range(2):
                    toks = slice((2 * half + tt) * P, (2 * half + tt + 1) * P)
                    mm = three(ps[:, SCORE, tt * W2:(tt + 1) * W2],
                               [(q_hi[:, toks], q_lo[:, toks], k_bd[:, 0, u, :], k_bd[:, 1, u, :])], True, True)
                mm.then_inc(s_s_mm, 1)

            def turn_z(b, t, bank):
                when(pe, s_zn, TT * (b - 1) + t + 1)
                for c in range(DC):
                    mm = pe.transpose(ps[:, bank, c * P:(c + 1) * P], zn[:, t % 2, c * P:(c + 1) * P], ident[:])
                mm.then_inc(s_zt_mm, 1)

            def feed_forward(b, t, bank):
                when(pe, s_zt_lo, TT * (b - 1) + t + 1)
                i = t % 2
                three(ps[:, bank, :], [(zt_hi[:, i, c, :], zt_lo[:, i, c, :], wf_hi[:, c, :], wf_lo[:, c, :])
                                       for c in range(DC)], True, True).then_inc(s_f_mm, 1)

            def weigh_values(b, u):
                g = b * NU + u
                vu = (u - 2) % NU
                when(pe, s_pt, 2 * (g - 1))
                if vu % HALF == 0:
                    vb = b if u >= 2 else b - 1
                    when(pe, s_v_in[vu // HALF], 16 * (vb + 1))
                    if isinstance(b, int) and b == 0:
                        pe.wait_ge(s_null_v, 16)
                for e in range(2):
                    cols = slice(vu * P + e * DH, vu * P + (e + 1) * DH)
                    mm = pe.matmul(ps[DH * e:DH * (e + 1), WORK + 1, :], v_sb[:, cols], p_t[:, e, :],
                                   start=True, stop=True)
                mm.then_inc(s_pv_mm, 1)

            def slot(b, u):
                cur, nxt, prev = has(b)
                g = b * NU + u
                pv, vu = unit_back(b, u, 2)
                yv, yu = unit_back(b, u, 3)
                if cur:
                    if nxt and x_slot(b, u) in (2, 4):
                        when(pe, s_xt_lo, TT * (b + 1) + {2: 1, 4: 4}[x_slot(b, u)])
                    if prev and u in (6, 7):
                        when(pe, s_zt_lo, TT * (b - 1) + u - 4)
                    if u == 0:
                        when(pe, s_xt_lo, TT * (b + 1))
                    par = b % 2
                    cols = slice(u * P, (u + 1) * P)
                    three(ps[:, WORK, :], [(wq_hi[:, c, cols], wq_lo[:, c, cols], xt_hi[:, par, c, :], xt_lo[:, par, c, :])
                                           for c in range(DC)], True, True).then_inc(s_q_mm, 1)
                late = V_LATE.get(u, ()) if isinstance(b, int) and b == 0 else ()
                if late:
                    if u != 1:
                        pe.wait_ge(s_v_act, 2 + u // 2)
                        pe.wait_ge(s_v_dve, 2 + u // 2)
                    values(late[0], (late[0] - 4) % 4)
                if pv:
                    when(pe, s_masked, 2 * g if cur else 2 * NU * B)
                    if not cur and not last_unit(b, u, 2):
                        when(pe, s_o_lo, g - 2)
                    when(pe, s_prob, g - 1)
                    for e in range(2):
                        for t in range(TT):
                            mm = pe.transpose(ps[0:JN, turned_bank(b, u) + e, t * P:(t + 1) * P],
                                              prob[:, u % 2, 2 * t + e, :], ident[:])
                        mm.then_inc(s_pt_mm, 1)
                if last_unit(b, u, 2):
                    when(pe, s_o_lo, g - 2)
                    weigh_values(b, u)
                if yv:
                    o = output_of(b, u, 3)
                    when(pe, s_o_lo, g - 2)
                    if yu % 2 == 0 and not (isinstance(b, int) and b > 1):
                        pe.wait_ge(s_w_lo, W_O + yu // 2 + 1)
                    for t in range(TT):
                        if yu == 0 and not (isinstance(b, int) and b == 0):
                            when(pe, s_y, TT * (b - 1) + t + 1)
                        toks = slice(t * P, (t + 1) * P)
                        three(ps[:, t, :], [(o[0][:, toks], o[1][:, toks], wo_hi[:, yu, :], wo_lo[:, yu, :])],
                              yu == 0, yu == NU - 1).then_inc(s_y_mm, 1)
                if cur:
                    if u % HALF == 0:
                        when(pe, s_k_lo[u // HALF], 2 * (b + 1))
                        if isinstance(b, int) and b == 0:
                            pe.wait_ge(s_null, 1)
                    if u < 2 and not pv:
                        when(pe, s_masked, 2 * g)
                    when(pe, s_q_lo, g + 1)
                    for t in X_TURN_5.get(x_slot(b, u), []) if nxt else []:
                        turn_x(b + 1, t, WORK)
                    if prev and u >= 5:
                        turn_z(b, u - 4, WORK)
                    scores(b, u, 0)
                if pv and not last_unit(b, u, 2):
                    weigh_values(b, u)
                if late:
                    values(late[1], (late[1] - 4) % 4)
                for t in X_TURN_7.get(x_slot(b, u), []) if nxt else []:
                    turn_x(b + 1, t, WORK + 2)
                if prev and u == 4:
                    turn_z(b, 0, WORK + 2)
                if prev and u >= 5:
                    if u == 5 and not (isinstance(b, int) and b > 1):
                        pe.wait_ge(s_w_lo, W_END)
                    if not (ends(b) and u - 5 in LATE_FF):
                        feed_forward(b, u - 5, WORK + 2)
                    if u == 7 and not ends(b):
                        when(pe, s_o_lo, g - 1)
                        feed_forward(b, 3, WORK + 1)
                if cur:
                    when(pe, s_masked, 2 * g + 1)
                    scores(b, u, 1)

            run(pe, slot)
            for t in LATE_FF:
                feed_forward(B - 1, t, WORK - 1 + t)
            turn_z(B, 0, SCORE)
            turn_z(B, 1, SCORE + 1)
            for t in range(TT):
                pe.wait_ge(s_yg, TT * (B - 1) + t + 1)
                feed_forward(B, t, t)
                if t == 1:
                    pe.wait_ge(s_res, TT * (B - 1))
                    turn_z(B, 2, SCORE + 2)
                    turn_z(B, 3, SCORE + 3)

        @block.scalar
        def _(act):
            def split_hi(n):
                hi, _, factor = parts_of(n)
                act.wait_ge(s_stage_in[n % 3], 16 * (n // 3 + 1))
                if n == W_Q:
                    act.wait_ge(s_gn_in, 16)
                if factor is None:
                    act.activation(hi, stage_of(n), ACT.Copy).then_inc(s_w_hi, 1)
                else:
                    act.activation(hi, stage_of(n), ACT.Copy, scale=factor).then_inc(s_w_hi, 1)

            def x_hi(b, t, bank):
                when(act, s_xt_mm, TT * b + t + 1)
                act.activation(xt_hi[:, b % 2, :, t * P:(t + 1) * P],
                               ps[:, bank, :].rearrange("p (c n) -> p c n", c=DC), ACT.Copy).then_inc(s_xt_hi, 1)

            act.dma_start(route[:, 0, :], ffn_logits.rearrange("(a e) -> a e", a=1)).then_inc(s_route_in, 16)
            act.dma_start(route[:, 1, :], ffn_u.rearrange("(a e) -> a e", a=1)).then_inc(s_route_in, 16)
            for c in range(CC):
                act.wait_ge(s_ctx_in[c], 16)
                act.activation(ctx_hi[:, c, :], ctx_in[:, c, :], ACT.Copy).then_inc(s_ctx_hi, 1)
                act.wait_ge(s_stage_in[c % 3], 16)
                act.activation(wk_hi[:, c, LEFT], stage[:, c % 3, LEFT], ACT.Copy).then_inc(s_wk_hi, 1)
                act.activation(wk_hi[:, c, RIGHT], stage[:, c % 3, RIGHT], ACT.Copy).then_inc(s_w_hi, 1)
            def values_left(n, bank):
                m, rows = value_rows(n)
                if m >= 2:
                    act.wait_ge(s_v_out[m % 2], 16 * (m // 2))
                act.wait_ge(s_v_mm, n + 1)
                act.activation(v_st[0:rows, m % 2, 0:512], ps[0:rows, bank, :], ACT.Copy).then_inc(s_v_act, 1)

            act.wait_ge(s_route_in, 32)
            act.activation(route[:, 2, :], route[:, 1, :], ACT.Ln).then_inc(s_ra, 1)
            act.wait_ge(s_ra, 1)
            act.activation(route[:, 3, :], route[:, 2, :], ACT.Ln, scale=-1.0).then_inc(s_ra, 1)
            act.wait_ge(s_rd, 1)
            act.activation(route[:, 4, :], route[:, 0, :], ACT.Exp, bias=route[:, 8, 0:1],
                           accum_out=route[:, 9, 0:1]).then_inc(s_ra, 1)
            act.wait_ge(s_ra, 3)
            act.activation(route[:, 9, 1:2], route[:, 9, 0:1], ACT.Ln).then_inc(s_ra, 1)
            act.wait_ge(s_const_in, 32)
            act.activation(tanh_g[:], gates[:], ACT.Tanh).then_inc(s_tanh, 1)
            for n in range(CC, CC + EARLY_V):
                split_hi(n)
            for j in range(2 * NU):
                c, h = j // 2, j % 2
                if h == 0:
                    if c >= KB:
                        act.wait_ge(s_k_out[c % KB], 16)
                    act.wait_ge(s_k_mm, j + 1)
                    act.activation(k_st[:, c % KB, 0:JH], ps[:, (j + 2) % 8, 0:JH], ACT.Copy,
                                   scale=DH ** -0.5).then_inc(s_k_act, 1)
                if j in KEY_SPLITS:
                    split_hi(KEY_SPLITS[j])
            for i, (kind, n) in enumerate(ring):
                if kind == "x":
                    x_hi(0, n, (i + 2) % 8)
                elif n % 2 == 0:
                    values_left(n, (i + 2) % 8)
            act.wait_ge(s_kz, 2)
            act.wait_ge(s_null_in, 32)
            for e in range(2):
                rows = slice(DH * e, DH * (e + 1))
                act.activation(k_bd[rows, 0, :, JN * e + J], null_k[rows, 0:1].to_broadcast([DH, NU]), ACT.Copy,
                               scale=DH ** -0.5).then_inc(s_null_hi, 1)

            def keys_hi(b, h):
                when(act, s_k_in[h], 16 * (b + 1))
                when(act, s_s_mm, 2 * (NU * (b - 1) + (h + 1) * HALF))
                for e in range(2):
                    rows = slice(DH * e, DH * (e + 1))
                    act.activation(k_bd[rows, 0, h * HALF:(h + 1) * HALF, JN * e:JN * e + J], k_raw[rows, h],
                                   ACT.Copy).then_inc(s_k_hi[h], 1)

            keys_hi(0, 0)

            def y_out(b, t):
                when(act, s_y_mm, TT * (b * NU - 1) + t + 1)
                act.activation(row[:, t, :], ps[:, t, :], ACT.Copy).then_inc(s_y, 1)

            def norm_z(b, t):
                when(act, s_z_nmr, TT * (b - 1) + t + 1)
                act.activation(zn[:, t % 2, :], row[:, t, :], ACT.Identity, bias=z_nmr[:, t:t + 1],
                               scale=z_rstd[:, t:t + 1]).then_inc(s_zn, 1)

            def z_hi(b, t, bank):
                when(act, s_zt_mm, TT * (b - 1) + t + 1)
                if t >= 2 or isinstance(b, int) and b == B:
                    when(act, s_f_mm, TT * (b - 1) + t - 1)
                act.activation(zt_hi[:, t % 2, :, :], ps[:, bank, :].rearrange("p (c n) -> p c n", c=DC),
                               ACT.Copy).then_inc(s_zt_hi, 1)

            def slot(b, u):
                cur, nxt, prev = has(b)
                g = b * NU + u
                sv, _ = unit_back(b, u, 1)
                pv, _ = unit_back(b, u, 2)
                if prev and u >= 5:
                    norm_z(b, u - 4)
                if cur:
                    when(act, s_s_mm, 2 * g)
                    when(act, s_q_mm, g + 1)
                    act.activation(q_hi[:], ps[:, WORK, :], ACT.Copy).then_inc(s_q_hi, 1)
                if sv:
                    when(act, s_sub, g)
                    i = (u - 1) % 2
                    act.activation(prob[:, i, :, :], prob[:, i, :, :], ACT.Exp).then_inc(s_exp, 1)
                if cur and u == 2:
                    keys_hi(b, 1)
                if nxt and u == NU - 1:
                    keys_hi(b + 1, 0)
                if isinstance(b, int) and b == 0 and u in V_LATE:
                    values_left(V_LATE[u][0], (V_LATE[u][0] - 4) % 4)
                if pv:
                    when(act, s_pv_mm, g - 2)
                    for e in range(2):
                        when(act, s_pt_mm, 2 * (g - 2) + e + 1)
                        act.activation(p_t[:, e, :], ps[0:JN, turned_bank(b, u) + e, :], ACT.Copy).then_inc(s_pt, 1)
                if prev and u == 4:
                    norm_z(b, 0)
                if prev and u == 2:
                    when(act, s_res_in, 16 * b)
                    for t in range(3):
                        y_out(b, t)
                for t in X_TURN_5.get(x_slot(b, u), []) if nxt else []:
                    x_hi(b + 1, t, WORK)
                if prev and u >= 5:
                    z_hi(b, u - 4, WORK)
                if pv:
                    if not last_unit(b, u, 2):
                        when(act, s_y_mm, TT * (g - 2))
                    when(act, s_pv_mm, g - 1)
                    act.activation(output_of(b, u, 2)[0][:], ps[:, WORK + 1, :], ACT.Copy).then_inc(s_o_hi, 1)
                for t in X_TURN_7.get(x_slot(b, u), []) if nxt else []:
                    x_hi(b + 1, t, WORK + 2)
                if prev and u == 4:
                    z_hi(b, 0, WORK + 2)
                if prev and u == 2:
                    y_out(b, 3)
                for n in splits_in(b, u):
                    if n == W_O + 2:
                        act.wait_ge(s_v_mm, 2 * VT)
                    split_hi(n)

            run(act, slot)
            norm_z(B, 0)
            norm_z(B, 1)
            z_hi(B, 0, SCORE)
            z_hi(B, 1, SCORE + 1)
            norm_z(B, 2)
            norm_z(B, 3)
            z_hi(B, 2, SCORE + 2)
            z_hi(B, 3, SCORE + 3)

        @block.vector
        def _(dve):
            def split_lo(n):
                hi, lo, factor = parts_of(n)
                dve.wait_ge(s_w_hi, n + 1)
                if factor is None:
                    dve.tensor_tensor(lo, stage_of(n), hi.bitcast(F32), ALU.subtract).then_inc(s_w_lo, 1)
                else:
                    dve.scalar_tensor_tensor(out=lo, in0=stage_of(n), scalar=factor, in1=hi.bitcast(F32),
                                             op0=ALU.mult, op1=ALU.subtract).then_inc(s_w_lo, 1)

            def after(semaphore, count):
                if not isinstance(count, int):
                    count = dve.snap(dve.to_reg(count))
                    dve.wait_ge(s_ctx_lo, 1)
                dve.wait_ge(semaphore, count)

            def x_stats(b, t):
                dve.wait_ge(s_x_in[t], 16 * (b + 1))
                dve.bn_stats(x_stat[:, t, :], xin[:, t, :]).then_inc(s_x_bn, 1)
                after(s_x_bn, TT * b + t + 1)
                dve.bn_aggr(x_mv[:, t, :], x_stat[:, t, :]).then_inc(s_x_mv, 1)
                dve.wait_ge(s_x_mv, TT * b + t + 1)
                dve.tensor_scalar(x_var[:, t:t + 1], x_mv[:, t, 1:2], 1.0 + EPS, EPS * EPS,
                                  ALU.mult, ALU.add).then_inc(s_x_var, 1)

            def x_norm(b, t):
                when(dve, s_x_rstd, TT * b + t + 1)
                dve.tensor_scalar(xin[:, t, :], xin[:, t, :], x_mv[:, t, 0:1], x_rstd[:, t:t + 1],
                                  ALU.subtract, ALU.mult).then_inc(s_xn, 1)

            def x_lo(b, t, bank):
                when(dve, s_xt_hi, TT * b + t + 1)
                cols = slice(t * P, (t + 1) * P)
                dve.tensor_tensor(xt_lo[:, b % 2, :, cols], ps[:, bank, :].rearrange("p (c n) -> p c n", c=DC),
                                  xt_hi[:, b % 2, :, cols].bitcast(F32), ALU.subtract).then_inc(s_xt_lo, 1)

            def values_right(n, bank):
                m, rows = value_rows(n)
                if m >= 2:
                    dve.wait_ge(s_v_out[m % 2], 16 * (m // 2))
                dve.wait_ge(s_v_mm, n + 1)
                dve.tensor_copy(v_st[0:rows, m % 2, 512:1024], ps[0:rows, bank, :]).then_inc(s_v_dve, 1)

            dve.memset(k_bd[:, 0].bitcast(F32), 0.0).then_inc(s_kz, 1)
            dve.memset(k_bd[:, 1].bitcast(F32), 0.0).then_inc(s_kz, 1)
            for c in range(CC):
                dve.wait_ge(s_ctx_hi, c + 1)
                dve.tensor_tensor(ctx_lo[:, c, :], ctx_in[:, c, :], ctx_hi[:, c, :].bitcast(F32),
                                  ALU.subtract).then_inc(s_ctx_lo, 1)
                for cols, hi_done, lo_done in ((LEFT, s_wk_hi, s_wk_lo), (RIGHT, s_w_hi, s_w_lo)):
                    dve.wait_ge(hi_done, c + 1)
                    dve.tensor_tensor(wk_lo[:, c, cols], stage[:, c % 3, cols], wk_hi[:, c, cols].bitcast(F32),
                                      ALU.subtract).then_inc(lo_done, 1)
                if c == CC - 1:
                    dve.wait_ge(s_route_in, 32)
                    dve.tensor_reduce(route[:, 8, 0:1], route[:, 0, :], AX.X, ALU.max, negate=True).then_inc(s_rd, 1)
            dve.memset(mask_bias[:], 0.0).then_inc(s_rd, 1)
            dve.wait_ge(s_ra, 4)
            dve.wait_ge(s_rd, 2)
            dve.tensor_scalar(route[:, 5, :], route[:, 0, :], route[:, 8, 0:1], route[:, 9, 1:2],
                              ALU.add, ALU.subtract).then_inc(s_rd, 1)
            dve.wait_ge(s_mask_in, 16)
            dve.tensor_scalar(mask_bias[:, :, 0:J], mask_u8[:].rearrange("p (b j) -> p b j", b=B), 1.0, MASKED,
                              ALU.subtract, ALU.mult).then_inc(s_mask, 1)
            dve.wait_ge(s_rd, 3)
            dve.tensor_tensor(route[:, 6, :], route[:, 5, :], route[:, 3, :], ALU.subtract).then_inc(s_rd, 1)
            dve.wait_ge(s_rd, 4)
            dve.max(route[:, 7, :], route[:, 6, :]).then_inc(s_rd, 1)
            dve.wait_ge(s_rd, 5)
            dve.max_index(route_i[:], route[:, 7, :], route[:, 6, :]).then_inc(s_expert, 1)
            for n in range(CC, CC + EARLY_V):
                split_lo(n)
            for j in range(2 * NU):
                c, h = j // 2, j % 2
                if h == 1:
                    if c >= KB:
                        dve.wait_ge(s_k_out[c % KB], 16)
                    dve.wait_ge(s_k_mm, j + 1)
                    dve.tensor_scalar(k_st[:, c % KB, JH:2 * JH], ps[:, (j + 2) % 8, 0:JH], DH ** -0.5, None,
                                      ALU.mult).then_inc(s_k_dve, 1)
                if j in KEY_SPLITS:
                    split_lo(KEY_SPLITS[j])
                for t in {5: [0, 1], 7: [2], 8: [3]}.get(j, []):
                    x_stats(0, t)
                for t in {8: [0, 1], 10: [2, 3]}.get(j, []):
                    x_norm(0, t)
            for i, (kind, n) in enumerate(ring):
                if kind == "x":
                    x_lo(0, n, (i + 2) % 8)
                elif n % 2 == 1:
                    values_right(n, (i + 2) % 8)
            dve.wait_ge(s_null_hi, 2)
            for e in range(2):
                rows = slice(DH * e, DH * (e + 1))
                nl = dve.scalar_tensor_tensor(out=k_bd[rows, 1, :, JN * e + J], in0=null_k[rows, 0:1].to_broadcast([DH, NU]),
                                              scalar=DH ** -0.5, in1=k_bd[rows, 0, :, JN * e + J].bitcast(F32),
                                              op0=ALU.mult, op1=ALU.subtract)
            nl.then_inc(s_null, 1)
            dve.wait_ge(s_gout_in, 16)
            dve.wait_ge(s_tanh, 1)
            dve.tensor_scalar(gout[:], gout[:], tanh_g[:, 0:1], None, ALU.mult)

            def keys_lo(b, h):
                for e in range(2):
                    rows = slice(DH * e, DH * (e + 1))
                    place = slice(h * HALF, (h + 1) * HALF), slice(JN * e, JN * e + J)
                    when(dve, s_k_hi[h], 2 * b + e + 1)
                    dve.tensor_tensor(k_bd[rows, 1, place[0], place[1]], k_raw[rows, h],
                                      k_bd[rows, 0, place[0], place[1]].bitcast(F32),
                                      ALU.subtract).then_inc(s_k_lo[h], 1)

            keys_lo(0, 0)

            def y_stats(b, tiles):
                for t in tiles:
                    when(dve, s_y, TT * (b - 1) + t + 1)
                    dve.bn_stats(y_stat[:, t, :], row[:, t, :]).then_inc(s_y_bn, 1)

            def y_aggregate(b, tiles):
                after(s_y_bn, TT * (b - 1) + tiles[-1] + 1)
                for t in tiles:
                    dve.bn_aggr(y_mv[:, t, :], y_stat[:, t, :]).then_inc(s_y_mv, 1)

            def y_variance(b, tiles):
                dve.wait_ge(s_y_mv, TT * (b - 1) + tiles[-1] + 1)
                span = slice(tiles[0], tiles[-1] + 1)
                dve.tensor_scalar(y_var[:, span], y_mv[:, span, 1], EPS, None, ALU.add).then_inc(s_y_var, 1)

            def y_gain(b, t, y):
                dve.scalar_tensor_tensor(out=row[:, t, :], in0=y, scalar=y_mv[:, t, 0:1], in1=gout[:],
                                         op0=ALU.subtract, op1=ALU.mult).then_inc(s_yg, 1)

            def x1(b, t, powers):
                when(dve, s_y_rstd, powers)
                dve.wait_ge(s_yg, TT * (b - 1) + t + 1)
                dve.scalar_tensor_tensor(out=row[:, t, :], in0=row[:, t, :], scalar=y_rstd[:, t:t + 1],
                                         in1=x_res[:, t, :], op0=ALU.mult, op1=ALU.add).then_inc(s_x1, 1)

            def z_stats(b, t):
                dve.wait_ge(s_x1, TT * (b - 1) + t + 1)
                dve.bn_stats(z_stat[:, t, :], row[:, t, :]).then_inc(s_z_bn, 1)

            def z_aggregate(b, t):
                after(s_z_bn, TT * (b - 1) + t + 1)
                dve.bn_aggr(z_mv[:, t, :], z_stat[:, t, :]).then_inc(s_z_mv, 1)

            def z_variance(b, t):
                dve.wait_ge(s_z_mv, TT * (b - 1) + t + 1)
                dve.tensor_scalar(z_var[:, t:t + 1], z_mv[:, t, 1:2], EPS, None, ALU.add).then_inc(s_z_var, 1)

            def x1_stats(b, t):
                z_stats(b, t)
                z_aggregate(b, t)
                z_variance(b, t)

            def z_shift(b, t):
                when(dve, s_z_rstd, TT * (b - 1) + t + 1)
                dve.scalar_tensor_tensor(out=z_nmr[:, t:t + 1], in0=z_mv[:, t, 0:1], scalar=-1.0,
                                         in1=z_rstd[:, t:t + 1], op0=ALU.mult, op1=ALU.mult).then_inc(s_z_nmr, 1)

            def z_lo(b, t, bank):
                when(dve, s_zt_hi, TT * (b - 1) + t + 1)
                dve.tensor_tensor(zt_lo[:, t % 2, :, :], ps[:, bank, :].rearrange("p (c n) -> p c n", c=DC),
                                  zt_hi[:, t % 2, :, :].bitcast(F32), ALU.subtract).then_inc(s_zt_lo, 1)

            def result(b, t, bank, to=row):
                when(dve, s_x1b, TT * (b - 1) + t + 1)
                when(dve, s_f_mm, TT * (b - 1) + t + 1)
                dve.tensor_tensor(to[:, t, :], ps[:, bank, :], row[:, t, :], ALU.add).then_inc(s_res, 1)

            def unmask(b, u, half):
                when(dve, s_s_mm, 2 * (b * NU + u) + half + 1)
                dve.tensor_tensor(prob[:, u % 2, 4 * half:4 * half + 4, :], psum_scores,
                                  mask_bias[:, bass.ds(b, 1), :].to_broadcast([P, 4, JN]),
                                  ALU.add).then_inc(s_masked, 1)

            def slot(b, u):
                cur, nxt, prev = has(b)
                g = b * NU + u
                sv, _ = unit_back(b, u, 1)
                pv, _ = unit_back(b, u, 2)
                if prev and u == 3:
                    y_stats(b, [2, 3])
                    y_aggregate(b, [0, 1, 2, 3])
                    y_variance(b, [0, 1, 2, 3])
                if prev and u == 4:
                    x1_stats(b, 0)
                if prev and u >= 5:
                    z_shift(b, u - 4)
                if prev and u in (4, 5, 6):
                    y_gain(b, u - 3, row[:, u - 3, :])
                    x1(b, u - 3, b)
                for t in X_NORM_A.get(x_slot(b, u), []) if nxt else []:
                    x_norm(b + 1, t)
                for t in X_STATS_A.get(x_slot(b, u), []) if nxt else []:
                    x_stats(b + 1, t)
                if sv and not cur:
                    dve.wait_ge(s_top_ok, g)
                    dve.tensor_tensor(prob[:, (u - 1) % 2, :, :], prob[:, (u - 1) % 2, :, :], spread(s_top[:]),
                                      ALU.subtract).then_inc(s_sub, 1)
                if cur:
                    when(dve, s_q_hi, g + 1)
                    dve.tensor_tensor(q_lo[:], ps[:, WORK, :], q_hi[:].bitcast(F32), ALU.subtract)\
                        .then_inc(s_q_lo, 1)
                if sv:
                    when(dve, s_exp, g)
                    dve.tensor_reduce(s_sum[:], prob[:, (u - 1) % 2, :, :], AX.X, ALU.add).then_inc(s_sum_ok, 1)
                    when(dve, s_sum_ok, g)
                    when(dve, s_prob, g - 1)
                    dve.reciprocal(s_rcp[:], s_sum[:]).then_inc(s_rcp_ok, 1)
                if sv and not cur:
                    dve.wait_ge(s_rcp_ok, g)
                    dve.tensor_tensor(prob[:, (u - 1) % 2, :, :], prob[:, (u - 1) % 2, :, :], spread(s_rcp[:]),
                                      ALU.mult).then_inc(s_prob, 1)
                if prev and u == 4:
                    z_shift(b, 0)
                if prev and u in (4, 5, 6):
                    x1_stats(b, u - 3)
                if prev and u == 3:
                    y_gain(b, 0, row[:, 0, :])
                    x1(b, 0, b)
                if cur and u == 2:
                    keys_lo(b, 1)
                if nxt and u == NU - 1:
                    keys_lo(b + 1, 0)
                for t in X_STATS_B.get(x_slot(b, u), []) if nxt else []:
                    x_stats(b + 1, t)
                for t in X_NORM_B.get(x_slot(b, u), []) if nxt else []:
                    x_norm(b + 1, t)
                if isinstance(b, int) and b == 0 and u == 5:
                    dve.wait_ge(s_bias_in, 16)
                    dve.tensor_scalar(bias[:], bias[:], tanh_g[:, 1:2], None, ALU.mult).then_inc(s_bias, 1)
                if cur:
                    if u == 0 and isinstance(b, int) and b == 0:
                        dve.wait_ge(s_mask, 1)
                    when(dve, s_pt_mm, 2 * (g - 1))
                    unmask(b, u, 0)
                if isinstance(b, int) and b == 0 and u in V_LATE:
                    values_right(V_LATE[u][1], (V_LATE[u][1] - 4) % 4)
                for t in X_TURN_5.get(x_slot(b, u), []) if nxt else []:
                    x_lo(b + 1, t, WORK)
                if prev and u >= 5:
                    z_lo(b, u - 4, WORK)
                if prev and u == 2:
                    y_stats(b, [0, 1])
                if pv:
                    when(dve, s_o_hi, g - 1)
                    hi, lo = output_of(b, u, 2)
                    dve.tensor_tensor(lo[:], ps[:, WORK + 1, :], hi[:].bitcast(F32), ALU.subtract)\
                        .then_inc(s_o_lo, 1)
                for t in X_TURN_7.get(x_slot(b, u), []) if nxt else []:
                    x_lo(b + 1, t, WORK + 2)
                if prev and u == 4:
                    z_lo(b, 0, WORK + 2)
                if prev and u >= 5 and not (ends(b) and u - 5 in LATE_FF):
                    result(b, u - 5, WORK + 2)
                if prev and u == 7 and not ends(b):
                    result(b, 3, WORK + 1)
                if cur:
                    unmask(b, u, 1)
                    when(dve, s_masked, 2 * g + 2)
                    dve.tensor_reduce(s_top[:], prob[:, u % 2, :, :], AX.X, ALU.max).then_inc(s_top_ok, 1)
                for n in splits_in(b, u):
                    split_lo(n)

            run(dve, slot)
            def y_stats_psum(t):
                dve.wait_ge(s_y_mm, TT * (B * NU - 1) + t + 1)
                dve.bn_stats(y_stat[:, t, :], ps[:, t, :]).then_inc(s_y_bn, 1)

            for t in (0, 2):
                n = t + 1
                if t == 0:
                    y_stats_psum(0)
                    y_stats_psum(1)
                y_aggregate(B, [t])
                y_aggregate(B, [n])
                if t:
                    result(B - 1, t, WORK - 1 + t, xin)
                y_variance(B, [t])
                if t == 0:
                    dve.wait_ge(s_res_in, 16 * B)
                else:
                    dve.wait_ge(s_res, TT * (B - 2) + t + 1)
                y_gain(B, t, ps[:, t, :])
                if t:
                    z_lo(B, 0, SCORE)
                    result(B - 1, n, WORK - 1 + n, xin)
                y_variance(B, [n])
                x1(B, t, B + t)
                if t:
                    dve.wait_ge(s_res, TT * (B - 2) + n + 1)
                y_gain(B, n, ps[:, n, :])
                if t:
                    z_lo(B, 1, SCORE + 1)
                z_stats(B, t)
                x1(B, n, B + n)
                z_aggregate(B, t)
                z_stats(B, n)
                z_variance(B, t)
                if t == 0:
                    y_stats_psum(2)
                z_aggregate(B, n)
                z_variance(B, n)
                z_shift(B, t)
                if t == 0:
                    y_stats_psum(3)
                if t:
                    result(B, 0, 0)
                z_shift(B, n)
            z_lo(B, 2, SCORE + 2)
            result(B, 1, 1)
            z_lo(B, 3, SCORE + 3)
            result(B, 2, 2)
            result(B, 3, 3)

        @block.gpsimd
        def _(pool):
            def x_power(b, t):
                when(pool, s_x_var, TT * b + t + 1)
                pool.tensor_tensor(x_rstd[:, t:t + 1], x_var[:, t:t + 1], half_neg[:, 0:1], ALU.pow)\
                    .then_inc(s_x_rstd, 1)

            def z_power(b, t):
                when(pool, s_z_var, TT * (b - 1) + t + 1)
                pool.tensor_tensor(z_rstd[:, t:t + 1], z_var[:, t:t + 1], half_neg[:, 0:1], ALU.pow)\
                    .then_inc(s_z_rstd, 1)

            def add_bias(b, t):
                when(pool, s_zn, TT * (b - 1) + t + 1)
                pool.tensor_tensor(row[:, t, :], row[:, t, :], bias[:], ALU.add).then_inc(s_x1b, 1)

            pool.dma_start(gates[:, 0:1], g_xattn.partition_broadcast(P)).then_inc(s_const_in, 16)
            pool.dma_start(gates[:, 1:2], g_ffn.partition_broadcast(P)).then_inc(s_const_in, 16)
            for e in range(2):
                pool.dma_start(null_k[DH * e:DH * (e + 1), :], null_kv[0].rearrange("(d o) -> d o", o=1))\
                    .then_inc(s_null_in, 16)
            pool.dma_start(v_sb[J:JN, :].rearrange("a (h d) -> a h d", d=DH),
                           null_kv[1:2, :].rearrange("a (h d) -> a h d", h=1).to_broadcast([1, INNER // DH, DH]))\
                .then_inc(s_null_v, 16)
            pool.dma_start(mask_u8[:], mask.rearrange("b j -> (b j)").partition_broadcast(P)).then_inc(s_mask_in, 16)
            pool.dma_start(gout[:], g_out.partition_broadcast(P)).then_inc(s_gout_in, 16)
            pool.memset(half_neg[:], -0.5)
            pool.memset(ident[:], 0.0).then_inc(s_ident, 1)
            pool.wait_ge(s_ident, 1)
            pool.affine_select(out=ident[:], in_=ident[:], compare_op=ALU.not_equal, fill=1.0, base=0,
                               pattern=[[-1, P]], channel_multiplier=1).then_inc(s_ident, 1)
            for t in range(TT):
                x_power(0, t)

            def slot(b, u):
                cur, nxt, prev = has(b)
                g = b * NU + u
                sv, _ = unit_back(b, u, 1)
                i = (u - 1) % 2
                if sv and cur:
                    when(pool, s_top_ok, g)
                    pool.tensor_tensor(prob[:, i, :, :], prob[:, i, :, :], spread(s_top[:]), ALU.subtract)\
                        .then_inc(s_sub, 1)
                if prev and u == 3:
                    when(pool, s_y_var, b)
                    pool.tensor_tensor(y_rstd[:], y_var[:], half_neg[:], ALU.pow).then_inc(s_y_rstd, 1)
                if prev and u == 4:
                    z_power(b, 0)
                if sv and cur:
                    when(pool, s_rcp_ok, g)
                    pool.tensor_tensor(prob[:, i, :, :], prob[:, i, :, :], spread(s_rcp[:]), ALU.mult)\
                        .then_inc(s_prob, 1)
                for t in {0: [0, 1], 1: [2, 3]}.get(x_slot(b, u), []) if nxt else []:
                    x_power(b + 1, t)
                if prev and u >= 4:
                    if u == 4 and not (isinstance(b, int) and b > 1):
                        pool.wait_ge(s_bias, 1)
                    add_bias(b, u - 4)
                if prev and 4 <= u < 7:
                    z_power(b, u - 3)

            run(pool, slot)
            def y_power(t):
                pool.wait_ge(s_y_var, B + t)
                pool.tensor_tensor(y_rstd[:, t:t + 1], y_var[:, t:t + 1], half_neg[:, 0:1], ALU.pow)\
                    .then_inc(s_y_rstd, 1)
            for t in (0, 2):
                y_power(t)
                y_power(t + 1)
                if t:
                    add_bias(B, t - 2)
                    add_bias(B, t - 1)
                z_power(B, t)
                z_power(B, t + 1)
            add_bias(B, 2)
            add_bias(B, 3)


_INS = ["x", "ctx_768", "mask_BxS2_bf1", "g_xattn", "g_ffn", "L0_xattn_g_norm", "L0_xattn_null_kv", "L0_xattn_Wq",
        "L0_xattn_Wkv", "L0_xattn_Wout", "L0_xattn_g_out", "L0_ffn_W", "L0_ffn_b", "L0_ffn_logits", "L0_ffn_u"]


def kernel(**inputs):
    import numpy as np
    import concourse.bacc as bacc
    from concourse import mybir as mb
    from concourse.bass_utils import run_bass_kernel_spmd

    nc = bacc.Bacc("TRN2", target_bir_lowering=False, num_devices=1)
    arrays, args = {}, []
    for name in _INS:
        a = np.asarray(inputs[name])
        if name == "ctx_768":
            a = a.reshape(-1, a.shape[-1]).T
        if name == "L0_xattn_g_norm":
            a = a.reshape(-1, P).T
        a = np.ascontiguousarray(a)
        if a.dtype == np.bool_:
            a = a.view(np.uint8)
        arrays[f"in_{name}"] = a
        args.append(nc.dram_tensor(f"in_{name}", a.shape, mb.dt.from_np(a.dtype), kind="ExternalInput").ap())
    shape = inputs["x"].shape
    args.append(nc.dram_tensor("out_0", shape, mb.dt.float32, kind="ExternalOutput").ap())
    flamingo_program(nc, *args)
    r = run_bass_kernel_spmd(nc, [arrays], core_ids=[0])
    return r.results[0]["out_0"]
```
